# Optimizing a Trainium2 kernel written in Bass

```python
import numpy as np
import jax
import jax.numpy as jnp

def _softmax(x, axis=-1):
    return jax.nn.softmax(x, axis=axis)
def _gelu(x):
    return jax.nn.gelu(x, approximate=True)
def _silu(x):
    return jax.nn.silu(x)
def _sigmoid(x):
    return jax.nn.sigmoid(x)
def _layernorm(x, axis=-1, eps=1e-5):
    m = jnp.mean(x, axis=axis, keepdims=True)
    v = jnp.var(x, axis=axis, keepdims=True)
    return (x - m) / jnp.sqrt(v + eps)
def _scatter_add(tgt, idx, src, axis=0):
    return tgt.at[idx].add(src)
def _segment_sum(src, seg, n):
    return jax.ops.segment_sum(src, seg, n)

kernel_name = 'mk_conv_preact_d2_conv_nchw512_317ef5'

def setup_inputs(seed: int = 0):
    np.random.seed(seed)
    _w = jnp.asarray
    def _rec_inputs():
        import jax
        import jax.numpy as jnp
        _gk = jax.random.key(seed)
        x = -0.0002928 + 1 * jax.random.normal(jax.random.fold_in(_gk, 1), (8, 512, 32, 32), jnp.float32)
        return x
    x = _rec_inputs()
    def _L0_conv_setup():
        import jax, jax.numpy as jnp
        import numpy as np
        B, C1, C2, N, F, HEADS, E = (8, 512, 512, 2, 32, 4, 0.5)
        C = int(C2 * E)
        HD = C // HEADS
        BN_EPS = 0.001

        def conv2d(x, w, pad):
            return jax.lax.conv_general_dilated(x, w, (1, 1), [(pad, pad), (pad, pad)], dimension_numbers=('NCHW', 'OIHW', 'NCHW'))

        def bn_eval(x, p):
            g, b, m, v = p
            s = (g / jnp.sqrt(v + BN_EPS))[:, None, None]
            return (x - m[:, None, None]) * s + b[:, None, None]

        def cbs(x, w, p, pad):
            return jax.nn.silu(bn_eval(conv2d(x, w, pad), p))

        def bot_attention(x, qkv_w, rw, rh):
            b, c, h, w = x.shape
            hw = h * w
            qkv = conv2d(x, qkv_w, 0).reshape(b, 3, HEADS, HD, hw)
            q, k, v = (qkv[:, 0], qkv[:, 1], qkv[:, 2])
            r = (rw + rh).reshape(1, HEADS, HD, hw)
            logits = jnp.einsum('bhdi,bhdj->bhij', q, k + r) * HD ** (-0.5)
            a = jax.nn.softmax(logits, axis=-1)
            out = jnp.einsum('bhij,bhdj->bhdi', a, v)
            return out.reshape(b, c, h, w)
        key = jax.random.key(seed)
        ks = iter(jax.random.split(key, 32))

        def nrm(shape, s=0.05):
            return jax.random.normal(next(ks), shape, jnp.float32) * s

        def bnp(cc):
            return jnp.stack([1.0 + 0.1 * jax.random.normal(next(ks), (cc,), jnp.float32), 0.1 * jax.random.normal(next(ks), (cc,), jnp.float32), 0.1 * jax.random.normal(next(ks), (cc,), jnp.float32), 0.5 + jax.random.uniform(next(ks), (cc,), jnp.float32)])
        return {'x': jax.random.normal(next(ks), (B, C1, F, F), jnp.float32), 'cv1_w': nrm((2 * C, C1, 1, 1)), 'cv1_bn': bnp(2 * C), 'cv2_w': nrm((C2, (2 + N) * C, 1, 1)), 'cv2_bn': bnp(C2), 'm_cv1_w': nrm((N, C, C, 3, 3)), 'm_cv1_bn': jnp.stack([bnp(C) for _ in range(N)]), 'm_qkv_w': nrm((N, 3 * C, C, 1, 1)), 'm_rw': jax.random.normal(next(ks), (N, 1, HEADS, HD, 1, F), jnp.float32), 'm_rh': jax.random.normal(next(ks), (N, 1, HEADS, HD, F, 1), jnp.float32), 'm_cv2_w': nrm((N, C, C, 1, 1)), 'm_cv2_bn': jnp.stack([bnp(C) for _ in range(N)])}
    _L0_conv_all = _L0_conv_setup()
    _L0_conv_in = {k: v for k, v in _L0_conv_all.items() if k in ('cv1_w', 'cv1_bn', 'cv2_w', 'cv2_bn', 'm_cv1_w', 'm_cv1_bn', 'm_qkv_w', 'm_rw', 'm_rh', 'm_cv2_w', 'm_cv2_bn', )}
    del _L0_conv_all

    def _L1_conv_setup():
        import jax, jax.numpy as jnp
        import numpy as np
        EPS = 0.0001
        GROUPS = 8

        def _whiten_group(cov):
            _, e, vh = jnp.linalg.svd(cov)
            v = vh.T
            L = e.shape[0]
            hit = e <= EPS
            counter = jnp.where(jnp.any(hit), jnp.argmax(hit) + 1, 1)
            keep = jnp.arange(L) < counter
            w = jnp.where(keep, jax.lax.rsqrt(e), 0.0)
            return v * w[None, :] @ v.T
        key = jax.random.key(seed)
        k1, k2 = jax.random.split(key)
        N, C, H, W = (64, 512, 32, 32)
        x = jax.random.normal(k1, (N, C, H, W), dtype=jnp.float32)
        weight = jax.random.uniform(k2, (C, 1), dtype=jnp.float32)
        bias = jnp.zeros((C, 1), dtype=jnp.float32)
        return {'x': x, 'weight': weight, 'bias': bias}
    _L1_conv_all = _L1_conv_setup()
    _L1_conv_in = {k: v for k, v in _L1_conv_all.items() if k in ('weight', 'bias', )}
    del _L1_conv_all

    return {
        "x": x,
        "L0_conv_cv1_w": _L0_conv_in["cv1_w"],
        "L0_conv_cv1_bn": _L0_conv_in["cv1_bn"],
        "L0_conv_cv2_w": _L0_conv_in["cv2_w"],
        "L0_conv_cv2_bn": _L0_conv_in["cv2_bn"],
        "L0_conv_m_cv1_w": _L0_conv_in["m_cv1_w"],
        "L0_conv_m_cv1_bn": _L0_conv_in["m_cv1_bn"],
        "L0_conv_m_qkv_w": _L0_conv_in["m_qkv_w"],
        "L0_conv_m_rw": _L0_conv_in["m_rw"],
        "L0_conv_m_rh": _L0_conv_in["m_rh"],
        "L0_conv_m_cv2_w": _L0_conv_in["m_cv2_w"],
        "L0_conv_m_cv2_bn": _L0_conv_in["m_cv2_bn"],
        "L1_conv_weight": _L1_conv_in["weight"],
        "L1_conv_bias": _L1_conv_in["bias"],
    }

def reference(x, L0_conv_cv1_w, L0_conv_cv1_bn, L0_conv_cv2_w, L0_conv_cv2_bn, L0_conv_m_cv1_w, L0_conv_m_cv1_bn, L0_conv_m_qkv_w, L0_conv_m_rw, L0_conv_m_rh, L0_conv_m_cv2_w, L0_conv_m_cv2_bn, L1_conv_weight, L1_conv_bias):
    import jax
    import jax.numpy as jnp
    def _L0_conv_ref(x, cv1_w, cv1_bn, cv2_w, cv2_bn, m_cv1_w, m_cv1_bn, m_qkv_w, m_rw, m_rh, m_cv2_w, m_cv2_bn):
        import jax, jax.numpy as jnp
        import numpy as np
        B, C1, C2, N, F, HEADS, E = (8, 512, 512, 2, 32, 4, 0.5)
        C = int(C2 * E)
        HD = C // HEADS
        BN_EPS = 0.001

        def conv2d(x, w, pad):
            return jax.lax.conv_general_dilated(x, w, (1, 1), [(pad, pad), (pad, pad)], dimension_numbers=('NCHW', 'OIHW', 'NCHW'))

        def bn_eval(x, p):
            g, b, m, v = p
            s = (g / jnp.sqrt(v + BN_EPS))[:, None, None]
            return (x - m[:, None, None]) * s + b[:, None, None]

        def cbs(x, w, p, pad):
            return jax.nn.silu(bn_eval(conv2d(x, w, pad), p))

        def bot_attention(x, qkv_w, rw, rh):
            b, c, h, w = x.shape
            hw = h * w
            qkv = conv2d(x, qkv_w, 0).reshape(b, 3, HEADS, HD, hw)
            q, k, v = (qkv[:, 0], qkv[:, 1], qkv[:, 2])
            r = (rw + rh).reshape(1, HEADS, HD, hw)
            logits = jnp.einsum('bhdi,bhdj->bhij', q, k + r) * HD ** (-0.5)
            a = jax.nn.softmax(logits, axis=-1)
            out = jnp.einsum('bhij,bhdj->bhdi', a, v)
            return out.reshape(b, c, h, w)
        t = cbs(x, cv1_w, cv1_bn, 0)
        ys = [t[:, :C], t[:, C:]]
        for i in range(N):
            yi = ys[-1]
            z = cbs(yi, m_cv1_w[i], m_cv1_bn[i], 1)
            z = bot_attention(z, m_qkv_w[i], m_rw[i], m_rh[i])
            z = jax.nn.silu(bn_eval(conv2d(z, m_cv2_w[i], 0), m_cv2_bn[i]))
            ys.append(yi + z)
        return cbs(jnp.concatenate(ys, axis=1), cv2_w, cv2_bn, 0)

    def _L1_conv_ref(x, weight, bias):
        import jax, jax.numpy as jnp
        import numpy as np
        EPS = 0.0001
        GROUPS = 8

        def _whiten_group(cov):
            _, e, vh = jnp.linalg.svd(cov)
            v = vh.T
            L = e.shape[0]
            hit = e <= EPS
            counter = jnp.where(jnp.any(hit), jnp.argmax(hit) + 1, 1)
            keep = jnp.arange(L) < counter
            w = jnp.where(keep, jax.lax.rsqrt(e), 0.0)
            return v * w[None, :] @ v.T
        N, C, H, W = x.shape
        G = GROUPS
        L = C // G
        M = N * H * W
        xf = jnp.transpose(x, (1, 0, 2, 3)).reshape(C, M)
        mu = xf.mean(1, keepdims=True)
        xc = xf - mu
        xg = xc.reshape(G, L, M)
        cov = jnp.einsum('glm,gkm->glk', xg, xg) / M + EPS * jnp.eye(L, dtype=xg.dtype)
        sub = jax.vmap(_whiten_group)(cov)
        xr = jnp.einsum('glk,gkm->glm', sub, xg).reshape(C, M)
        xr = xr * weight + bias
        return jnp.transpose(xr.reshape(C, N, H, W), (1, 0, 2, 3))

    def _gn(v, G=32, eps=1e-5):
        B_, C_, H_, W_ = v.shape
        g = v.reshape(B_, G, C_ // G, H_, W_)
        m = jnp.mean(g, axis=(2, 3, 4), keepdims=True)
        s = jnp.var(g, axis=(2, 3, 4), keepdims=True)
        return ((g - m) / jnp.sqrt(s + eps)).reshape(v.shape)

    def _ln_c(v, eps=1e-6):
        m = jnp.mean(v, axis=1, keepdims=True)
        s = jnp.var(v, axis=1, keepdims=True)
        return (v - m) / jnp.sqrt(s + eps)

    def _ln_t(v, eps=1e-5):
        m = jnp.mean(v, axis=-1, keepdims=True)
        s = jnp.var(v, axis=-1, keepdims=True)
        return (v - m) / jnp.sqrt(s + eps)

    def _to_tokens(v):
        B_, C_, H_, W_ = v.shape
        return v.reshape(B_, C_, H_ * W_).transpose(0, 2, 1)
    def _from_tokens(t, like):
        B_, C_, H_, W_ = like.shape
        return t.transpose(0, 2, 1).reshape(B_, C_, H_, W_)

    x = x + _L0_conv_ref(_gn(x), L0_conv_cv1_w, L0_conv_cv1_bn, L0_conv_cv2_w, L0_conv_cv2_bn, L0_conv_m_cv1_w, L0_conv_m_cv1_bn, L0_conv_m_qkv_w, L0_conv_m_rw, L0_conv_m_rh, L0_conv_m_cv2_w, L0_conv_m_cv2_bn)
    x = x + _L1_conv_ref(_gn(x), L1_conv_weight, L1_conv_bias)
    return x


_drawn_inputs = setup_inputs


def setup_inputs(seed=0):
    import zlib

    import numpy as np

    out = dict(_drawn_inputs(seed))
    spreads = {'L1_conv_bias': (0.0, 0.1)}
    factors = {}
    for name, (base, spread) in spreads.items():
        noise = np.random.default_rng([zlib.crc32(name.encode()), seed]).standard_normal(out[name].shape)
        drawn = base * np.exp(spread * noise) if base else spread * noise
        out[name] = jnp.asarray(drawn.astype(out[name].dtype))
    for name, factor in factors.items():
        out[name] = (out[name] * factor).astype(out[name].dtype)
    return out
```

```python
from contextlib import ExitStack

import concourse.bass as bass
from concourse import mybir

F32 = mybir.dt.float32
F16 = mybir.dt.float16
ALU = mybir.AluOpType
ACT = mybir.ActivationFunctionType
AX = mybir.AxisListType

P = 128
B, C, F = 8, 512, 32
HW = F * F
CH = C // 2
N = 2
HEADS, HD = 4, 64
TC, TH = C // P, CH // P
PF = F + 2
TAPS = 9
NT = HW // P
HALF = 512
WSCALE = 64.0
BN_EPS, GN_EPS, COV_EPS = 1e-3, 1e-5, 1e-4
PSHIFT = 8 * 0.6931471805599453
MSCALE = 64.0
VW = 2 * HD + 1

W_CV1 = 0
W_M = W_CV1 + TC * C
W_QKV = W_M + N * TAPS * TH * CH
W_PROJ = W_QKV + N * TH * 3 * CH
W_CV2 = W_PROJ + N * TH * CH
W_END = W_CV2 + (2 + N) * TH * C
WCHUNK = 1024
WCHUNKS = W_END // WCHUNK

BN_CV1, BN_M, BN_PROJ, BN_CV2 = 0, TC, TC + N * TH, TC + 2 * N * TH
NBN = 2 * TC + 2 * N * TH

J_STAT0 = 0
J_CV1 = J_STAT0 + TC
J_MOD = J_CV1 + TC
JM_CONV, JM_Q, JM_K, JM_V, JM_AOT, JM_PROJ, JM = 0, 2, 4, 6, 8, 10, 12
J_CV2 = J_MOD + N * JM
J_STAT1 = J_CV2 + TC
J_TR = J_STAT1 + TC
J_GRAM = J_TR + TC
JOBS = J_GRAM + TC
A_JOBS = ([J_CV1 + t for t in range(TC)] + [J_MOD + n * JM + k for n in range(N) for k in range(JM)]
          + [J_CV2 + t for t in range(TC)] + [J_TR + t for t in range(TC)])
ACTS = len(A_JOBS)
STEPS = HEADS * NT
ATT = N * STEPS
PRIME = 4
SQUARINGS = 3
ROUNDS = 8
PER_ROUND_DVE = 2 * SQUARINGS + 2
PER_ROUND_PE = 3 * SQUARINGS + 1
DVE_SETUP_CHAIN = 26
DVE_IMAGE_CHAIN = 124
DVE_ROUND_CHAIN = 9


def spread(ap, dim, n):
    ap = ap.unsqueeze(dim)
    return ap.broadcast_to([n if i == dim else k for i, k in enumerate(ap.shape)])


def build(nc, x, w_all, bn, rw_in, rh_in, consts, l1w, l1b, out):
    x1d = nc.dram_tensor("x1_scratch", (B, TC, P, HW), F32).ap()
    x_v = x.rearrange("b (t p) h w -> b t p (h w)", p=P)
    out_v = out.rearrange("b (t p) h w -> b t p (h w)", p=P)
    ctx = ExitStack()
    with ctx:
        def sb(name, shape, dt):
            return ctx.enter_context(nc.sbuf_tensor(name, shape, dt))

        def sem(name):
            return ctx.enter_context(nc.semaphore(name))

        WH = sb("w_hi", [P, W_END], F16)
        WL = sb("w_lo", [P, W_END], F16)
        X = sb("x_tiles", [P, TC, HW], F32)
        Y0 = sb("y0", [P, 2, TH, HW], F16)
        YP = sb("y_padded", [P, N + 1, 2, TH, PF, PF], F16)
        Z = sb("z", [P, 2, TH, HW], F16)
        SH = sb("shared", [P, TC, 2, HW], F16)
        Q3 = sb("q3", [P, HEADS, HW], F16)
        K2 = sb("k2", [P, HEADS, HW], F16)
        V = sb("v", [P, NT, HEADS, VW + 1], F16)
        R4 = sb("ring", [P, 4, HW], F32)
        AO = sb("attn_out", [P, NT, CH], F32)
        CST = sb("consts", [P, 4, P], F32)
        BNR = sb("bn_raw", [P, 4, NBN], F32)
        BNS = sb("bn_scale", [P, NBN], F32)
        BNB = sb("bn_bias", [P, NBN], F32)
        RW = sb("rw", [P, N, TH, F], F32)
        RH = sb("rh", [P, N, TH, F], F32)
        LW = sb("l1_w", [P, TC], F32)
        LB = sb("l1_b", [P, TC], F32)
        HALFNEG = sb("minus_half", [P, NBN], F32)
        SHIFT = sb("shift", [P, 1], F32)
        BST = sb("bn_stats", [P, TC, 2, 6], F32)
        MV = sb("mean_var", [P, TC, 2], F32)
        ST = sb("mean_sq", [P, TC, 2], F32)
        GS = sb("group_mean_sq", [P, TC, 2], F32)
        VAR = sb("group_var", [P, TC], F32)
        RST = sb("rstd", [P, TC], F32)
        NB = sb("norm_bias", [P, TC], F32)
        NM = sb("minus_max", [P, HEADS * NT], F32)
        NMT = sb("minus_max_t", [HEADS * NT, P], F16)
        RC = sb("recip", [P, NT], F32)
        COV = sb("cov", [P, TC, P], F32)
        MU = sb("mu", [P, TC], F32)
        RSB = sb("rstd_of_images", [P, B + 1, TC], F32)
        NBB = sb("norm_bias_of_images", [P, B, TC], F32)

        ps = ctx.enter_context(nc.psum_tensor("ps", [P, 8, HALF], F32))

        def pair(j):
            return ps[:, 2 * (j % 4):2 * (j % 4) + 2, :].rearrange("p a n -> p (a n)")

        ident, avg16, ones64, ones = (CST[:, i, :] for i in range(4))
        XN = SH[:, :, :, :].rearrange("p t s n -> p s t n")
        Q2 = SH[:, :, 0, :]
        K1 = SH[:, :, 1, :]
        YT = SH[:, :, :, :].rearrange("p t s n -> p t (s n)").bitcast(F32).rearrange("p t (a c) -> p t a c", c=P)
        STAGE = SH[:, :, :, :].rearrange("p t s n -> p t (s n)").bitcast(F32)
        U = R4[:, 0:2, :]
        T = R4[:, 2:4, :]
        PF32 = R4[:, 0:2, :]
        PHL = R4[:, 2:4, :].bitcast(F16).rearrange("p r (s n) -> p r s n", s=2)
        NORM = R4[:, :, :]

        def w2(Wt, base, k, width, lo, n):
            return Wt[:, base + k * width + lo:base + k * width + lo + n]

        wloaded = [sem(f"weights_loaded{i}") for i in range(4)]
        wsplit = sem("weights_split")
        small_loaded = sem("small_loaded")
        setup_pool = sem("setup_pool")
        setup_dve = sem("setup_done")
        x_loaded = [sem(f"x_loaded{i}") for i in range(TC)]
        x1_stored = sem("x1_stored")
        job_done = sem("job_done")
        act_done = sem("act_done")
        drained = sem("drained")
        stat_ready = sem("stat_ready")
        var_ready = sem("var_ready")
        rstd_ready = sem("rstd_ready")
        mx_done = sem("max_logits_done")
        mx_used = sem("max_taken")
        nmt_done = sem("max_transposed")
        nmt_ready = sem("max_row_ready")
        aug_loaded = sem("max_row_placed")
        qk_done = sem("logits_done")
        exp_done = sem("exp_done")
        ph_done = sem("p_hi_done")
        pl_done = sem("p_lo_done")
        pv_done = sem("pv_done")
        o_used = sem("head_output_taken")
        chain = sem("dve_chain")
        l1_loaded = [sem(f"x1_loaded{i}") for i in range(4)]
        l1_stored = [sem(f"out_stored{i}") for i in range(4)]
        fin_pe = sem("fin_pe")
        fin_dve = sem("fin_dve")
        fin_stage = sem("fin_stage")
        fin_pool = sem("fin_pool")
        ap_done = sem("applied")
        ap_used = sem("applied_taken")
        mat_ready = sem("matrices_ready")

        block = ctx.enter_context(nc.Block())

        L1 = R4[:, :, :].rearrange("p r (t c) -> p r t c", t=8)
        BC = AO[:, :, :].rearrange("p a c -> p (a c)").rearrange("p (i t c) -> p i t c", i=4, t=4)
        Zf = Z[:, :, :, :].rearrange("p s t n -> p (s t n)").bitcast(F32).rearrange("p (i t c) -> p i t c", i=4, t=4)
        V4 = Y0[:, :, :, :].rearrange("p s t n -> p (s t n)").bitcast(F32)
        A_, Bm, Cm, W_ = (BC[:, i, :, :] for i in range(4))
        NY, NZ, NTm, SUB = (Zf[:, i, :, :] for i in range(4))
        SCR = L1[:, 0, 0:TC, :]
        MASKS = V4[:, 0:P]
        TR = V4[:, P:P + 8]
        IV = V4[:, P + 8:P + 16]
        DG = V4[:, P + 16:P + 24]
        EV = V4[:, P + 24:P + 40]
        CB = V4[:, P + 64:P + 64 + TC * B].rearrange("p (t b) -> p t b", t=TC)
        MB = V4[:, P + 128:P + 128 + TC * B].rearrange("p (t b) -> p t b", t=TC)
        LIN = SH[:, :, :, :].rearrange("p t s n -> p t (s n)").bitcast(F32)
        LOUT = X[:, :, :]
        SB = WH[:, 0:2 * 4 * 2 * P].bitcast(F32).rearrange("p (r c) -> p r c", c=P)

        def fin_pe_part(pe, mm):
            def blocks(dst, lhs, rhs):
                for t in range(TC):
                    ins = mm(dst[:, t * P:(t + 1) * P], lhs(t), rhs[:, t, :], start=True, stop=True)
                return ins

            def of(m):
                return lambda t: m[:, t, :]

            def all_ones(t):
                return ones
            pe.wait_ge(fin_stage, 1)
            blocks(pair(0), all_ones, SCR).then_inc(fin_pe, 1)
            pe.wait_ge(fin_stage, 2)
            mm(pair(1)[:, 0:TC], ones64, DG[:, 0:TC], start=True, stop=True).then_inc(fin_pe, 1)
            pe.wait_ge(fin_stage, 3)
            with pe.Fori(0, ROUNDS) as r:
                for k in range(SQUARINGS):
                    base = 3 + r * PER_ROUND_DVE + k * 2
                    pe.wait_ge(fin_stage, base)
                    blocks(pair(0), of(Bm), Bm)
                    blocks(pair(0)[:, HALF:], of(Cm), Cm).then_inc(fin_pe, 1)
                    blocks(pair(1), of(NZ), NY).then_inc(fin_pe, 1)
                    pe.wait_ge(fin_stage, base + 1)
                    blocks(pair(2), of(NY), NTm)
                    blocks(pair(2)[:, HALF:], of(NTm), NZ).then_inc(fin_pe, 1)
                pe.wait_ge(fin_stage, 3 + r * PER_ROUND_DVE + 2 * SQUARINGS + 1)
                mm(pair(3)[:, 0:8], ones64, DG[:, 0:8], start=True, stop=True).then_inc(fin_pe, 1)
            last = 3 + ROUNDS * PER_ROUND_DVE
            pe.wait_ge(fin_stage, last + 1)
            mm(pair(3)[:, 0:8], ones64, DG[:, 0:8], start=True, stop=True).then_inc(fin_pe, 1)
            pe.wait_ge(fin_stage, last + 2)
            blocks(pair(0), all_ones, SCR).then_inc(fin_pe, 1)
            pe.wait_ge(fin_stage, last + 3)
            for t in range(TC):
                ins = mm(pair(1)[:, t * B:(t + 1) * B], SUB[:, t, :], MB[:, t, :], start=True, stop=True)
            ins.then_inc(fin_pe, 1)

        @block.sync
        def _(sp):
            for dst, src in ((CST[:, :, :], consts), (BNR[:, :, :], bn), (RW[:, :, :, :], rw_in),
                             (RH[:, :, :, :], rh_in), (LW[:, :], l1w), (LB[:, :], l1b)):
                sp.dma_start(dst, src).then_inc(small_loaded, 16)
            for c in range(WCHUNKS):
                if c >= 4:
                    sp.wait_ge(wsplit, c - 3)
                sp.dma_start(STAGE[:, c % 4, :], w_all[:, c * WCHUNK:(c + 1) * WCHUNK]).then_inc(wloaded[c % 4], 16)
            for t in range(TC):
                sp.dma_start(X[:, t, :], x_v[0, t, :, :]).then_inc(x_loaded[t], 16)

            def image(b, last, following=None):
                for n in range(N):
                    sp.wait_ge(nmt_ready, b * N + n + 1)
                    sp.dma_start(Q3[HD:HD + 1, :, :], NMT[:, :]).then_inc(aug_loaded, 16)
                for t in range(TC):
                    sp.wait_ge(drained, b * JOBS + PRIME + J_CV2 + t + 1)
                    sp.dma_start(x1d[b, t, :, :], X[:, t, :]).then_inc(x1_stored, 16)
                if not last:
                    sp.wait_ge(drained, b * JOBS + PRIME + J_STAT1 + TC)
                sp.wait_ge(x1_stored, b * 16 * TC + 16 * TC)
                if not last:
                    for t in range(TC):
                        sp.dma_start(X[:, t, :], x_v[following, t, :, :]).then_inc(x_loaded[t], 16)

            with sp.Fori(1, B) as following:
                image(following - 1, False, following)
            image(B - 1, True)
            with sp.Fori(0, B) as b:
                for t in range(TC):
                    sp.wait_ge(ap_used, b * TC + t + 1)
                    sp.dma_start(LIN[:, t, :], x1d[b, t, :, :]).then_inc(l1_loaded[t], 16)
            for t in range(TC):
                sp.wait_ge(l1_stored[t], 16 * B + 16)

        @block.gpsimd
        def _(pool):
            g = nc.gpsimd
            g.memset(YP[:, :, :, :, :, :], 0.0).then_inc(setup_pool, 1)
            pool.wait_ge(setup_pool, 1)
            g.memset(K2[HD:HD + 1, :, :], MSCALE).then_inc(setup_pool, 1)
            pool.wait_ge(setup_pool, 2)
            g.memset(V[:, :, :, :], 1.0).then_inc(setup_pool, 1)
            pool.wait_ge(setup_pool, 3)
            g.memset(HALFNEG[:, :], -0.5).then_inc(setup_pool, 1)
            pool.wait_ge(setup_pool, 4)
            g.memset(SHIFT[:, :], PSHIFT).then_inc(setup_pool, 1)
            pool.wait_ge(setup_pool, 5)
            pool.wait_ge(chain, 1)
            g.tensor_tensor(BNS[:, :], BNR[:, 3, :], HALFNEG[:, :], ALU.pow).then_inc(setup_pool, 1)

            def rstds(b, base, which):
                for t in range(TC):
                    pool.wait_ge(var_ready, b * 2 * TC + base + t + 1)
                    g.tensor_tensor(RST[:, t:t + 1], VAR[:, t:t + 1], HALFNEG[:, 0:1], ALU.pow).then_inc(rstd_ready, 1)

            with pool.Fori(0, B) as b:
                rstds(b, 0, 0)
                rstds(b, TC, 1)
            pool.wait_ge(fin_dve, 1)
            g.tensor_tensor(EV[:, 8:16], EV[:, 0:8], HALFNEG[:, 0:8], ALU.pow).then_inc(fin_pool, 1)

        @block.scalar
        def _(act):
            a = nc.scalar

            def silu_part(b, j, col):
                act.wait_ge(job_done, b * JOBS + j + 1)
                act.wait_ge(drained, b * JOBS + j + PRIME - 1)
                a.activation(U[:, j % 2, :], pair(j), ACT.Identity, bias=BNB[:, col:col + 1], scale=BNS[:, col:col + 1])
                a.activation(T[:, j % 2, :], pair(j), ACT.Tanh, bias=BNB[:, col:col + 1],
                             scale=BNS[:, col:col + 1]).then_inc(act_done, 1)

            act.wait_ge(setup_dve, 1)
            with act.Fori(0, B) as b:
                for t in range(TC):
                    silu_part(b, J_CV1 + t, BN_CV1 + t)
                for n in range(N):
                    jm = J_MOD + n * JM
                    for t in range(TH):
                        silu_part(b, jm + JM_CONV + t, BN_M + n * TH + t)
                    for t in range(TH):
                        j = jm + JM_Q + t
                        act.wait_ge(job_done, b * JOBS + j + 1)
                        for e in range(2):
                            r = slice(e * HD, (e + 1) * HD)
                            ins = a.activation(Q2[r, 2 * t + e, :], pair(j)[r, :], ACT.Copy, scale=1.0 / WSCALE)
                        ins.then_inc(act_done, 1)
                    for t in range(TH):
                        j = jm + JM_K + t
                        act.wait_ge(job_done, b * JOBS + j + 1)
                        act.wait_ge(drained, b * JOBS + j + PRIME - 1)
                        a.activation(U[:, j % 2, :], pair(j), ACT.Copy, scale=1.0 / WSCALE).then_inc(act_done, 1)
                    act.wait_ge(nmt_done, b * N + n + 1)
                    a.activation(NMT[:, :], ps[0:HEADS * NT, 0, 0:P], ACT.Copy, scale=1.0 / MSCALE).then_inc(nmt_ready, 1)
                    for t in range(2):
                        j = jm + JM_V + t
                        act.wait_ge(job_done, b * JOBS + j + 1)
                        a.activation(V[:, 4 * t:4 * t + 4, :, 0:HD],
                                     pair(j).rearrange("p (i h d) -> p i h d", i=4, h=HEADS), ACT.Copy,
                                     scale=1.0 / WSCALE).then_inc(act_done, 1)
                    for s in range(STEPS):
                        g = b * ATT + n * STEPS + s
                        act.wait_ge(qk_done, g + 1)
                        act.wait_ge(pl_done, g + 1)
                        a.activation(PF32[:, s % 2, :], pair(s % 2), ACT.Exp, bias=SHIFT[:, 0:1],
                                     scale=HD ** -0.5).then_inc(exp_done, 1)
                    for t in range(TH):
                        j = jm + JM_AOT + t
                        act.wait_ge(job_done, b * JOBS + j + 1)
                        a.activation(Z[:, 0, t, :], pair(j), ACT.Copy).then_inc(act_done, 1)
                    for t in range(TH):
                        silu_part(b, jm + JM_PROJ + t, BN_PROJ + n * TH + t)
                for t in range(TC):
                    silu_part(b, J_CV2 + t, BN_CV2 + t)
                for t in range(TC):
                    act.wait_ge(job_done, b * JOBS + J_TR + t + 1)
                    a.activation(YT[:, t, 0:NT // 2, :].rearrange("p a c -> p (a c)"), pair(J_TR + t)[:, 0:HALF], ACT.Copy)\
                        .then_inc(act_done, 1)
            with act.Fori(0, B) as b:
                for t in range(TC):
                    act.wait_ge(ap_used, b * TC + t + 1 + 4)
                    act.dma_start(out_v[b, t, :, :], LOUT[:, t, :]).then_inc(l1_stored[t], 16)

        @block.tensor
        def _(pe):
            mm = nc.tensor.matmul

            def begin(b, j):
                pe.wait_ge(drained, b * JOBS + PRIME + j - 3)

            def products(j, parts, rhs_of, first=True):
                o = pair(j)
                last = len(parts) - 1
                for i, (w, key) in enumerate(parts):
                    for h in range(2):
                        ins = mm(o[:, h * HALF:(h + 1) * HALF], w, rhs_of(key, h), start=(i == 0), stop=(i == last))
                ins.then_inc(job_done, 1)

            def three(w_hi, w_lo, key):
                return [(w_hi, (0, key)), (w_hi, (1, key)), (w_lo, (0, key))]

            pe.wait_ge(setup_dve, 1)
            with pe.Fori(0, B) as b:
                for t in range(TC):
                    begin(b, J_STAT0 + t)
                    pe.wait_ge(stat_ready, b * 2 * TC + t + 1)
                    mm(pair(J_STAT0 + t)[:, 0:2], avg16, ST[:, t, :], start=True, stop=True).then_inc(job_done, 1)
                pe.wait_ge(drained, b * JOBS + PRIME + J_STAT0 + TC)
                for t in range(TC):
                    begin(b, J_CV1 + t)
                    parts = []
                    for k in range(TC):
                        parts += three(w2(WH, W_CV1, k, C, t * P, P), w2(WL, W_CV1, k, C, t * P, P), k)
                    products(J_CV1 + t, parts, lambda key, h: XN[:, key[0], key[1], h * HALF:(h + 1) * HALF])
                for n in range(N):
                    jm = J_MOD + n * JM
                    pe.wait_ge(drained, b * JOBS + PRIME + jm)
                    for t in range(TH):
                        begin(b, jm + JM_CONV + t)
                        parts = []
                        for k in range(TH):
                            for tap in range(TAPS):
                                base = W_M + (n * TAPS + tap) * TH * CH
                                parts += three(w2(WH, base, k, CH, t * P, P), w2(WL, base, k, CH, t * P, P), (k, tap))

                        def shifted(key, h):
                            hl, (k, tap) = key
                            dy, dx = tap // 3, tap % 3
                            y0 = dy + h * (F // 2)
                            return YP[:, n, hl, k, y0:y0 + F // 2, dx:dx + F]
                        products(jm + JM_CONV + t, parts, shifted)
                    pe.wait_ge(drained, b * JOBS + PRIME + jm + JM_Q)
                    zr = lambda key, h: Z[:, key[0], key[1], h * HALF:(h + 1) * HALF]
                    wq = W_QKV + n * TH * 3 * CH
                    for m in range(2 * TH):
                        begin(b, jm + JM_Q + m)
                        parts = []
                        for k in range(TH):
                            parts += three(w2(WH, wq, k, 3 * CH, m * P, P), w2(WL, wq, k, 3 * CH, m * P, P), k)
                        products(jm + JM_Q + m, parts, zr)
                    pe.wait_ge(drained, b * JOBS + PRIME + jm + JM_V)
                    for s in range(STEPS):
                        h, i = s // NT, s % NT
                        if s >= 4:
                            pe.wait_ge(mx_used, b * ATT + n * STEPS + s - 3)
                        for e in range(2):
                            ins = mm(pair(s)[:, e * HALF:(e + 1) * HALF], Q2[:, h, i * P:(i + 1) * P],
                                     K1[:, h, e * HALF:(e + 1) * HALF], start=True, stop=True)
                        ins.then_inc(mx_done, 1)
                    pe.wait_ge(mx_used, b * ATT + (n + 1) * STEPS)
                    nc.tensor.transpose(ps[0:HEADS * NT, 0, 0:P], NM[:, :], ident).then_inc(nmt_done, 1)
                    for t in range(2):
                        j = jm + JM_V + t
                        begin(b, j)
                        for i in range(4):
                            pos = (4 * t + i) * P
                            o = pair(j)[:, i * CH:(i + 1) * CH]
                            for k in range(TH):
                                zh, zl = Z[:, 0, k, pos:pos + P], Z[:, 1, k, pos:pos + P]
                                vh, vl = w2(WH, wq, k, 3 * CH, 2 * CH, CH), w2(WL, wq, k, 3 * CH, 2 * CH, CH)
                                mm(o, zh, vh, start=(k == 0), stop=False)
                                mm(o, zh, vl, start=False, stop=False)
                                ins = mm(o, zl, vh, start=False, stop=(k == TH - 1))
                        ins.then_inc(job_done, 1)
                    pe.wait_ge(drained, b * JOBS + PRIME + jm + JM_AOT)
                    pe.wait_ge(aug_loaded, b * 16 * N + 16 * (n + 1))

                    def logits(s):
                        h, i = s // NT, s % NT
                        keys = slice(i * P, (i + 1) * P)
                        if s >= 2:
                            pe.wait_ge(exp_done, b * ATT + n * STEPS + s - 1)
                        o = pair(s % 2)
                        for e in range(2):
                            mm(o[:, e * HALF:(e + 1) * HALF], K1[:, h, keys], Q2[:, h, e * HALF:(e + 1) * HALF],
                               start=True, stop=False)
                        for e in range(2):
                            ins = mm(o[:, e * HALF:(e + 1) * HALF], K2[0:HD + 1, h, keys],
                                     Q3[0:HD + 1, h, e * HALF:(e + 1) * HALF], start=False, stop=True)
                        ins.then_inc(qk_done, 1)

                    def values(s):
                        h, i = s // NT, s % NT
                        pe.wait_ge(pl_done, b * ATT + n * STEPS + s + 3)
                        if i == 0:
                            pe.wait_ge(o_used, (b * N + n) * HEADS + h + 1)
                        vh1, vl, last = V[:, i, h, 0:HD + 1], V[:, i, h, HD + 1:VW], i == NT - 1
                        for q in range(NT):
                            o = ps[:, 6 + q // 4, (q % 4) * P:(q % 4) * P + HD + 1]
                            ph = PHL[:, s % 2, 0, q * P:(q + 1) * P]
                            pl = PHL[:, s % 2, 1, q * P:(q + 1) * P]
                            mm(o, ph, vh1, start=(i == 0 and q % 4 == 0), stop=False, skip_group_check=True)
                            mm(o[:, 0:HD], ph, vl, start=False, stop=False, skip_group_check=True)
                            ins = mm(o, pl, vh1, start=False, stop=last, skip_group_check=True)
                        ins.then_inc(pv_done, 1)

                    logits(0)
                    logits(1)
                    for s in range(STEPS):
                        if s + 2 < STEPS:
                            logits(s + 2)
                        values(s)
                    pe.wait_ge(o_used, (b * N + n + 1) * HEADS + 1)
                    for t in range(TH):
                        j = jm + JM_AOT + t
                        for i in range(NT):
                            ins = nc.tensor.transpose(pair(j)[:, i * P:(i + 1) * P], AO[:, i, t * P:(t + 1) * P], ident)
                        ins.then_inc(job_done, 1)
                    pe.wait_ge(drained, b * JOBS + PRIME + jm + JM_PROJ)
                    wp = W_PROJ + n * TH * CH
                    for t in range(TH):
                        begin(b, jm + JM_PROJ + t)
                        parts = []
                        for k in range(TH):
                            parts += three(w2(WH, wp, k, CH, t * P, P), w2(WL, wp, k, CH, t * P, P), k)
                        products(jm + JM_PROJ + t, parts, zr)
                pe.wait_ge(drained, b * JOBS + PRIME + J_CV2)

                def joined(key, h):
                    hl, k = key
                    if k < TH:
                        return Y0[:, hl, k, h * HALF:(h + 1) * HALF]
                    y0 = 1 + h * (F // 2)
                    return YP[:, k // TH - 1, hl, k % TH, y0:y0 + F // 2, 1:1 + F]
                for t in range(TC):
                    begin(b, J_CV2 + t)
                    parts = []
                    for k in range((2 + N) * TH):
                        parts += three(w2(WH, W_CV2, k, C, t * P, P), w2(WL, W_CV2, k, C, t * P, P), k)
                    products(J_CV2 + t, parts, joined)
                for t in range(TC):
                    begin(b, J_STAT1 + t)
                    pe.wait_ge(stat_ready, b * 2 * TC + TC + t + 1)
                    mm(pair(J_STAT1 + t)[:, 0:2], avg16, ST[:, t, :], start=True, stop=True).then_inc(job_done, 1)
                for t in range(TC):
                    pe.wait_ge(drained, b * JOBS + PRIME + J_STAT1 + t + 1)
                    for i in range(NT):
                        ins = nc.tensor.transpose(pair(J_TR + t)[:, i * P:(i + 1) * P], NORM[:, t, i * P:(i + 1) * P],
                                                  ident)
                    ins.then_inc(job_done, 1)
                for t in range(TC):
                    pe.wait_ge(drained, b * JOBS + PRIME + J_TR + t + 1)
                    for i in range(NT):
                        ins = mm(pair(J_GRAM + t)[:, 0:P], YT[:, t, i, :], YT[:, t, i, :],
                                 start=(i == 0), stop=(i == NT - 1))
                    ins.then_inc(job_done, 1)

            fin_pe_part(pe, mm)
            with pe.Fori(0, B) as b:
                for t in range(TC):
                    pe.wait_ge(l1_loaded[t], 16 * b + 16)
                    pe.wait_ge(mat_ready, b * TC + t + 1)
                    for h in range(2):
                        ins = mm(pair(t)[:, h * HALF:(h + 1) * HALF], SB[:, t, :], LIN[:, t, h * HALF:(h + 1) * HALF],
                                 start=True, stop=True)
                    ins.then_inc(ap_done, 1)


        @block.vector
        def _(dve):
            v = nc.vector

            class Own:
                base, n = 0, 0

                def __call__(self, ins):
                    ins.then_inc(chain, 1)
                    self.n += 1
                    dve.wait_ge(chain, self.base + self.n)
            own = Own()

            v.memset(RC[:, 0:1], 0.0).then_inc(drained, PRIME)
            v.memset(RC[:, 1:2], 0.0).then_inc(pl_done, 2)
            v.memset(RC[:, 2:3], 0.0).then_inc(pv_done, 2)
            v.memset(RC[:, 3:4], 0.0).then_inc(o_used, 1)
            dve.wait_ge(small_loaded, 6 * 16)
            own(v.tensor_scalar(BNR[:, 3, :], BNR[:, 3, :], BN_EPS, None, ALU.add))
            dve.wait_ge(setup_pool, 6)
            own(v.tensor_tensor(BNS[:, :], BNS[:, :], BNR[:, 0, :], ALU.mult))
            own(v.tensor_tensor(BNB[:, :], BNR[:, 2, :], BNS[:, :], ALU.mult))
            own(v.tensor_tensor(BNB[:, :], BNR[:, 1, :], BNB[:, :], ALU.subtract))
            own(v.tensor_scalar(BNB[:, :], BNB[:, :], 0.5, None, ALU.mult))
            own(v.tensor_scalar(BNS[:, :], BNS[:, :], 0.5 / WSCALE, None, ALU.mult))
            for c in range(WCHUNKS):
                cols = slice(c * WCHUNK, (c + 1) * WCHUNK)
                dve.wait_ge(wloaded[c % 4], 16 * (c // 4 + 1))
                own(v.tensor_scalar(WH[:, cols], STAGE[:, c % 4, :], WSCALE, None, ALU.mult))
                v.scalar_tensor_tensor(WL[:, cols], STAGE[:, c % 4, :], WSCALE, WH[:, cols], ALU.mult,
                                       ALU.subtract).then_inc(wsplit, 1)
            v.memset(RSB[:, :, :], 0.0)
            v.memset(MU[:, :], 0.0)
            own(v.memset(COV[:, :, :], 0.0))
            v.memset(NM[:, 0:1], 0.0).then_inc(setup_dve, 1)
            assert own.n == DVE_SETUP_CHAIN, ("set-up", own.n)

            def split(hi, lo, src):
                own(v.tensor_copy(hi, src))
                return v.tensor_tensor(lo, src, hi, ALU.subtract)

            with dve.Fori(0, B) as b:
                own.base, own.n = b * DVE_IMAGE_CHAIN + DVE_SETUP_CHAIN, 0

                def drain(ins):
                    ins.then_inc(drained, 1)

                def normalise(base, job, finish):
                    def stats(t):
                        if base == 0:
                            dve.wait_ge(x_loaded[t], b * 16 + 16)
                        v.bn_stats(BST[:, t, 0, :], X[:, t, 0:HALF])
                        return v.bn_stats(BST[:, t, 1, :], X[:, t, HALF:])

                    def joined_stats(t):
                        return v.bn_aggr(MV[:, t, :], BST[:, t, :, :].rearrange("p a s -> p (a s)"))

                    def mean_and_square(t):
                        v.tensor_copy(ST[:, t, 0:1], MV[:, t, 0:1])
                        v.scalar_tensor_tensor(ST[:, t, 1:2], MV[:, t, 0:1], MV[:, t, 0:1], MV[:, t, 1:2], ALU.mult,
                                               ALU.add).then_inc(stat_ready, 1)
                    own(stats(0))
                    own(stats(1))
                    stats(2)
                    joined_stats(0)
                    joined_stats(1)
                    own(stats(3))
                    mean_and_square(0)
                    mean_and_square(1)
                    joined_stats(2)
                    own(joined_stats(3))
                    mean_and_square(2)
                    mean_and_square(3)
                    for t in range(TC):
                        dve.wait_ge(job_done, b * JOBS + job + t + 1)
                        own(v.tensor_copy(GS[:, t, :], pair(job + t)[:, 0:2]))
                        own(v.scalar_tensor_tensor(VAR[:, t:t + 1], GS[:, t, 0:1], GS[:, t, 0:1], GS[:, t, 1:2],
                                                   ALU.mult, ALU.subtract))
                        v.tensor_scalar(VAR[:, t:t + 1], VAR[:, t:t + 1], -1.0, GN_EPS, ALU.mult, ALU.add)\
                            .then_inc(var_ready, 1)
                    for t in range(TC):
                        dve.wait_ge(rstd_ready, b * 2 * TC + base + t + 1)
                        own(v.scalar_tensor_tensor(NB[:, t:t + 1], GS[:, t, 0:1], -1.0, RST[:, t:t + 1], ALU.mult,
                                                   ALU.mult))
                        own(v.tensor_scalar(NORM[:, t, :], X[:, t, :], RST[:, t:t + 1], NB[:, t:t + 1], ALU.mult,
                                            ALU.add))
                        drain(finish(t))

                def silu(j):
                    dve.wait_ge(act_done, b * ACTS + A_JOBS.index(j) + 1)
                    u = U[:, j % 2, :]
                    own(v.scalar_tensor_tensor(u, T[:, j % 2, :], 1.0, u, ALU.add, ALU.mult))
                    return u

                def padded(n, hl, t):
                    return YP[:, n, hl, t, 1:1 + F, 1:1 + F]

                def square(m):
                    return m.rearrange("p (y x) -> p y x", x=F)

                normalise(0, J_STAT0, lambda t: split(XN[:, 0, t, :], XN[:, 1, t, :], NORM[:, t, :]))
                for t in range(TC):
                    u = silu(J_CV1 + t)
                    if t < TH:
                        drain(split(Y0[:, 0, t, :], Y0[:, 1, t, :], u))
                    else:
                        drain(split(padded(0, 0, t - TH), padded(0, 1, t - TH), square(u)))
                for n in range(N):
                    jm = J_MOD + n * JM
                    for t in range(TH):
                        drain(split(Z[:, 0, t, :], Z[:, 1, t, :], silu(jm + JM_CONV + t)))
                    for t in range(TH):
                        j = jm + JM_Q + t
                        dve.wait_ge(act_done, b * ACTS + A_JOBS.index(j) + 1)
                        for e in range(2):
                            r, o = slice(e * HD, (e + 1) * HD), slice((1 - e) * HD, (2 - e) * HD)
                            v.tensor_copy(Q2[o, 2 * t + e, :], Q2[r, 2 * t + e, :])
                            ins = v.scalar_tensor_tensor(Q3[0:HD, 2 * t + e, :], pair(j)[r, :], 1.0 / WSCALE,
                                                         Q2[r, 2 * t + e, :], ALU.mult, ALU.subtract)
                        drain(ins)
                    for t in range(TH):
                        j = jm + JM_K + t
                        dve.wait_ge(act_done, b * ACTS + A_JOBS.index(j) + 1)
                        u = square(U[:, j % 2, :])
                        own(v.tensor_tensor(u, u, spread(RW[:, n, t, :], 1, F), ALU.add))
                        own(v.tensor_tensor(u, u, spread(RH[:, n, t, :], 2, F), ALU.add))
                        u = U[:, j % 2, :]
                        for e in range(2):
                            r, h = slice(e * HD, (e + 1) * HD), 2 * t + e
                            own(v.tensor_copy(K1[r, h, :], u[r, :]))
                            if e == 1:
                                v.tensor_copy(K1[0:HD, h, :], K1[r, h, :])
                            own(v.tensor_copy(K2[0:HD, h, :], K1[r, h, :]))
                            ins = v.tensor_tensor(K1[HD:P, h, :], u[r, :], K1[r, h, :], ALU.subtract)
                        drain(ins)
                    for s in range(STEPS):
                        dve.wait_ge(mx_done, b * ATT + n * STEPS + s + 1)
                        v.tensor_reduce(NM[:, s:s + 1], pair(s), AX.X, ALU.max, negate=True).then_inc(mx_used, 1)
                    for t in range(2):
                        j = jm + JM_V + t
                        dve.wait_ge(act_done, b * ACTS + A_JOBS.index(j) + 1)
                        drain(v.scalar_tensor_tensor(V[:, 4 * t:4 * t + 4, :, HD + 1:VW],
                                                     pair(j).rearrange("p (i h d) -> p i h d", i=4, h=HEADS),
                                                     1.0 / WSCALE, V[:, 4 * t:4 * t + 4, :, 0:HD], ALU.mult,
                                                     ALU.subtract))

                    def head_output(h):
                        dve.wait_ge(pv_done, b * ATT + n * STEPS + (h + 1) * NT + 2)
                        o = ps[:, 6:8, :].rearrange("p a (q d) -> p (a q) d", d=P)
                        own(v.reciprocal(RC[:, :].unsqueeze(2), o[:, :, HD:HD + 1]))
                        v.tensor_tensor(AO[:, :, h * HD:(h + 1) * HD], o[:, :, 0:HD],
                                        spread(RC[:, :], 2, HD), ALU.mult).then_inc(o_used, 1)

                    for s in range(STEPS):
                        dve.wait_ge(exp_done, b * ATT + n * STEPS + s + 1)
                        dve.wait_ge(pv_done, b * ATT + n * STEPS + s + 1)
                        v.tensor_copy(PHL[:, s % 2, 0, :], PF32[:, s % 2, :]).then_inc(ph_done, 1)
                        dve.wait_ge(ph_done, b * ATT + n * STEPS + s + 1)
                        v.tensor_tensor(PHL[:, s % 2, 1, :], PF32[:, s % 2, :], PHL[:, s % 2, 0, :],
                                        ALU.subtract).then_inc(pl_done, 1)
                        if s % NT == 0 and s:
                            head_output(s // NT - 1)
                    head_output(HEADS - 1)
                    for t in range(TH):
                        j = jm + JM_AOT + t
                        dve.wait_ge(act_done, b * ACTS + A_JOBS.index(j) + 1)
                        drain(v.tensor_tensor(Z[:, 1, t, :], pair(j), Z[:, 0, t, :], ALU.subtract))
                    for t in range(TH):
                        u = square(silu(jm + JM_PROJ + t))
                        own(v.tensor_tensor(u, u, padded(n, 0, t), ALU.add))
                        own(v.tensor_tensor(u, u, padded(n, 1, t), ALU.add))
                        drain(split(padded(n + 1, 0, t), padded(n + 1, 1, t), u))
                for t in range(TC):
                    u = silu(J_CV2 + t)
                    drain(v.tensor_tensor(X[:, t, :], X[:, t, :], u, ALU.add))

                def into_mean(t):
                    own(v.tensor_copy(RSB[:, b, t:t + 1], RST[:, t:t + 1]))
                    own(v.tensor_copy(NBB[:, b, t:t + 1], NB[:, t:t + 1]))
                    own(v.tensor_scalar(MV[:, t, 0:1], MV[:, t, 0:1], RST[:, t:t + 1], NB[:, t:t + 1], ALU.mult,
                                        ALU.add))
                    return v.tensor_tensor(MU[:, t:t + 1], MU[:, t:t + 1], MV[:, t, 0:1], ALU.add)
                normalise(TC, J_STAT1, into_mean)
                for t in range(TC):
                    dve.wait_ge(act_done, b * ACTS + A_JOBS.index(J_TR + t) + 1)
                    drain(v.tensor_copy(YT[:, t, NT // 2:, :].rearrange("p a c -> p (a c)"), pair(J_TR + t)[:, HALF:]))
                for t in range(TC):
                    dve.wait_ge(job_done, b * JOBS + J_GRAM + t + 1)
                    drain(v.tensor_tensor(COV[:, t, :], pair(J_GRAM + t)[:, 0:P], COV[:, t, :], ALU.add))
                assert own.n == DVE_IMAGE_CHAIN, ("image", own.n)

            own.base, own.n = DVE_SETUP_CHAIN + B * DVE_IMAGE_CHAIN, 0
            own(v.memset(TR[:, :], 0.0))
            for t in range(TC):
                v.memset(TR[:, TC + t:TC + t + 1], 0.0).then_inc(l1_stored[t], 16)
            v.memset(TR[:, 0:1], 0.0).then_inc(ap_used, 4)
            own(v.tensor_scalar(MU[:, :], MU[:, :], 1.0 / B, None, ALU.mult))

            def stage(ins):
                ins.then_inc(fin_stage, 1)

            def tiles(m):
                return m.rearrange("p (t c) -> p t c", c=P)

            def along(s, n=P):
                return spread(s, 2, n)

            def each(m):
                return spread(m, 1, TC)

            stage(v.tensor_tensor(SCR, each(ident), along(MU[:, :]), ALU.mult))
            dve.wait_ge(fin_pe, 1)
            own(v.tensor_tensor(W_, tiles(pair(0)[:, 0:HALF]), along(MU[:, :]), ALU.mult))
            own(v.scalar_tensor_tensor(A_, COV[:, :, :], 1.0 / (B * HW), W_, ALU.mult, ALU.subtract))
            own(v.tensor_tensor(A_, A_, each(ones64), ALU.mult))
            own(v.scalar_tensor_tensor(A_, each(ident), COV_EPS, A_, ALU.mult, ALU.add))
            own(v.tensor_tensor(SCR, A_, each(ident), ALU.mult))
            stage(v.tensor_reduce(DG[:, 0:TC], SCR, AX.X, ALU.add))
            dve.wait_ge(fin_pe, 2)
            own(v.tensor_copy(TR[:, 0:TC], pair(1)[:, 0:TC]))
            own(v.reciprocal(IV[:, 0:TC], TR[:, 0:TC]))
            own(v.tensor_tensor(Bm, A_, along(IV[:, 0:TC]), ALU.mult))
            own(v.scalar_tensor_tensor(Cm, Bm, -1.0, each(ident), ALU.mult, ALU.add))
            v.tensor_scalar(Cm, Cm, 1.0 / 64, None, ALU.mult)
            v.tensor_copy(NY, Bm)
            stage(v.tensor_copy(NZ, each(ident)))

            fin_chain = own.base + own.n
            with dve.Fori(0, ROUNDS) as r:
                own.base, own.n = fin_chain + r * DVE_ROUND_CHAIN, 0
                for k in range(SQUARINGS):
                    done = 2 + r * PER_ROUND_PE + 3 * k
                    dve.wait_ge(fin_pe, done + 2)
                    own(v.tensor_scalar(NTm, tiles(pair(1)[:, 0:HALF]), -0.5, None, ALU.mult))
                    stage(v.scalar_tensor_tensor(NTm, each(ident), 1.5, NTm, ALU.mult, ALU.add))
                    v.tensor_copy(Bm, tiles(pair(0)[:, 0:HALF]))
                    v.tensor_copy(Cm, tiles(pair(0)[:, HALF:]))
                    dve.wait_ge(fin_pe, done + 3)
                    v.tensor_copy(NY, tiles(pair(2)[:, 0:HALF]))
                    stage(v.tensor_copy(NZ, tiles(pair(2)[:, HALF:])))
                own(v.memset(EV[:, 0:1], 0.0))
                own(v.tensor_tensor(SCR, Bm, each(ident), ALU.mult))
                own(v.tensor_reduce(DG[:, 0:TC], SCR, AX.X, ALU.add))
                own(v.tensor_tensor(SCR, Cm, each(ident), ALU.mult))
                stage(v.tensor_reduce(DG[:, TC:2 * TC], SCR, AX.X, ALU.add))
                dve.wait_ge(fin_pe, 2 + (r + 1) * PER_ROUND_PE)
                own(v.reciprocal(IV[:, :], pair(3)[:, 0:2 * TC]))
                own(v.tensor_tensor(Bm, Bm, along(IV[:, 0:TC]), ALU.mult))
                stage(v.tensor_tensor(Cm, Cm, along(IV[:, TC:]), ALU.mult))
                assert own.n == DVE_ROUND_CHAIN, ("round", own.n)
            own.base, own.n = fin_chain + ROUNDS * DVE_ROUND_CHAIN, 0
            pe_done = 2 + ROUNDS * PER_ROUND_PE
            own(v.tensor_tensor(SCR, A_, Bm, ALU.mult))
            own(v.tensor_reduce(DG[:, 0:TC], SCR, AX.X, ALU.add))
            own(v.tensor_tensor(SCR, A_, Cm, ALU.mult))
            stage(v.tensor_reduce(DG[:, TC:2 * TC], SCR, AX.X, ALU.add))
            dve.wait_ge(fin_pe, pe_done + 1)
            own(v.tensor_scalar(IV[:, 0:TC], pair(3)[:, TC:2 * TC], COV_EPS, None, ALU.is_le))
            own(v.tensor_scalar(IV[:, TC:], IV[:, 0:TC], -1.0, 1.0, ALU.mult, ALU.add))
            v.tensor_copy(EV[:, TC:2 * TC], TR[:, 0:TC])
            v.tensor_copy(EV[:, 0:TC], pair(3)[:, 0:TC]).then_inc(fin_dve, 1)
            dve.wait_ge(fin_pool, 1)
            own(v.tensor_tensor(DG[:, 0:TC], EV[:, 2 * TC:3 * TC], IV[:, TC:], ALU.mult))
            own(v.tensor_tensor(DG[:, TC:2 * TC], EV[:, 3 * TC:], IV[:, 0:TC], ALU.mult))
            own(v.tensor_tensor(W_, Bm, along(DG[:, 0:TC]), ALU.mult))
            own(v.tensor_tensor(SUB, NZ, along(DG[:, TC:2 * TC]), ALU.mult))
            own(v.tensor_tensor(SUB, SUB, W_, ALU.add))
            stage(v.tensor_tensor(SCR, each(ident), along(LW[:, :]), ALU.mult))
            for t in range(TC):
                v.tensor_scalar(MB[:, t, :], NBB[:, :, t], -1.0, MU[:, t:t + 1], ALU.mult, ALU.add)
            dve.wait_ge(fin_pe, pe_done + 2)
            own(v.tensor_tensor(SUB, tiles(pair(0)[:, 0:HALF]), SUB, ALU.mult))
            stage(v.memset(EV[:, 0:1], 0.0))
            dve.wait_ge(fin_pe, pe_done + 3)
            for t in range(TC):
                ins = v.tensor_scalar(CB[:, t, :], pair(1)[:, t * B:(t + 1) * B], -1.0, LB[:, t:t + 1], ALU.mult,
                                      ALU.add)
            own(ins)
            for t in range(TC):
                v.tensor_scalar(SB[:, t, :], SUB[:, t, :], RSB[:, 0, t:t + 1], None, ALU.mult).then_inc(mat_ready, 1)
            with dve.Fori(0, B) as b:
                for t in range(TC):
                    dve.wait_ge(ap_done, b * TC + t + 1)
                    dve.wait_ge(l1_stored[t], b * 16 + 16)
                    v.scalar_tensor_tensor(LOUT[:, t, :], pair(t), CB[:, t, bass.ds(b, 1)], LIN[:, t, :], ALU.add,
                                           ALU.add).then_inc(ap_used, 1)
                    v.tensor_scalar(SB[:, t, :], SUB[:, t, :], RSB[:, b + 1, t:t + 1], None, ALU.mult)\
                        .then_inc(mat_ready, 1)


_INS = ("x", "w_all", "bn", "rw", "rh", "consts", "l1w", "l1b")


def kernel(x, L0_conv_cv1_w, L0_conv_cv1_bn, L0_conv_cv2_w, L0_conv_cv2_bn, L0_conv_m_cv1_w, L0_conv_m_cv1_bn,
           L0_conv_m_qkv_w, L0_conv_m_rw, L0_conv_m_rh, L0_conv_m_cv2_w, L0_conv_m_cv2_bn, L1_conv_weight,
           L1_conv_bias):
    import numpy as np
    import concourse.bacc as bacc
    from concourse.bass_utils import run_bass_kernel_spmd

    def turned(w):
        o, i = w.shape
        return w.reshape(o, i // P, P).transpose(2, 1, 0).reshape(P, -1)

    cv1, cv2, mc, qkv, mp = (np.asarray(a) for a in (L0_conv_cv1_w, L0_conv_cv2_w, L0_conv_m_cv1_w, L0_conv_m_qkv_w,
                                                     L0_conv_m_cv2_w))
    parts = [turned(cv1[:, :, 0, 0])]
    parts += [turned(mc[n, :, :, tap // 3, tap % 3]) for n in range(N) for tap in range(TAPS)]
    parts += [turned(qkv[n, :, :, 0, 0]) for n in range(N)]
    parts += [turned(mp[n, :, :, 0, 0]) for n in range(N)]
    parts += [turned(cv2[:, :, 0, 0])]
    w_all = np.ascontiguousarray(np.concatenate(parts, axis=1))
    bn1, bn2, bm, bp = (np.asarray(a) for a in (L0_conv_cv1_bn, L0_conv_cv2_bn, L0_conv_m_cv1_bn, L0_conv_m_cv2_bn))
    bn = np.concatenate([bn1, bm.transpose(1, 0, 2).reshape(4, -1), bp.transpose(1, 0, 2).reshape(4, -1), bn2], axis=1)
    bn = np.ascontiguousarray(bn.reshape(4, NBN, P).transpose(2, 0, 1))

    def heads(r):
        return np.ascontiguousarray(np.asarray(r).reshape(N, TH, P, F).transpose(2, 0, 1, 3))
    i = np.arange(P)
    consts = np.stack([np.eye(P), (i[:, None] // 16 == i[None] // 16) / 16.0, i[:, None] // 64 == i[None] // 64,
                       np.ones((P, P))], axis=1).astype(np.float32)
    arrays = dict(x=np.ascontiguousarray(x), w_all=w_all, bn=bn, rw=heads(L0_conv_m_rw), rh=heads(L0_conv_m_rh),
                  consts=np.ascontiguousarray(consts),
                  l1w=np.ascontiguousarray(np.asarray(L1_conv_weight).reshape(TC, P).T),
                  l1b=np.ascontiguousarray(np.asarray(L1_conv_bias).reshape(TC, P).T))
    nc = bacc.Bacc("TRN2", target_bir_lowering=False, num_devices=1)
    args = [nc.dram_tensor("in_" + k, arrays[k].shape, F32, kind="ExternalInput").ap() for k in _INS]
    out = nc.dram_tensor("out", (B, C, F, F), F32, kind="ExternalOutput").ap()
    build(nc, *args, out)
    r = run_bass_kernel_spmd(nc, [{"in_" + k: arrays[k] for k in _INS}], core_ids=[0])
    return r.results[0]["out"]
```

```python
from contextlib import ExitStack

import concourse.bass as bass
from concourse import mybir

F32 = mybir.dt.float32
F16 = mybir.dt.float16
ALU = mybir.AluOpType
ACT = mybir.ActivationFunctionType
AX = mybir.AxisListType

P = 128
B, C, F = 8, 512, 32
HW = F * F
CH = C // 2
N = 2
HEADS, HD = 4, 64
TC, TH = C // P, CH // P
PF = F + 2
TAPS = 9
NT = HW // P
HALF = 512
WSCALE = 64.0
BN_EPS, GN_EPS, COV_EPS = 1e-3, 1e-5, 1e-4
PSHIFT = 8 * 0.6931471805599453
MSCALE = 64.0
VW = 2 * HD + 1

W_CV1 = 0
W_M = W_CV1 + TC * C
W_QKV = W_M + N * TAPS * TH * CH
W_PROJ = W_QKV + N * TH * 3 * CH
W_CV2 = W_PROJ + N * TH * CH
W_END = W_CV2 + (2 + N) * TH * C
WCHUNK = 1024
WCHUNKS = W_END // WCHUNK

BN_CV1, BN_M, BN_PROJ, BN_CV2 = 0, TC, TC + N * TH, TC + 2 * N * TH
NBN = 2 * TC + 2 * N * TH

def plan(last):
    jobs = [(kind, 0, t) for kind in ("conv", "q", "k", "v", "aot", "proj") for t in range(TH)]
    jobs += [("conv", 1, t) for t in range(TH)]
    jobs += [] if last else [("stat0", 0, t) for t in range(TC)]
    jobs += [(kind, 1, t) for kind in ("q", "k", "v", "aot", "proj") for t in range(TH)]
    jobs += [("cv2", 0, t) for t in range(TC)]
    jobs += [] if last else [("cv1", 0, t) for t in range(2)]
    jobs += [("stat1", 0, t) for t in range(TC)]
    jobs += [] if last else [("cv1", 0, t) for t in range(2, TC)]
    jobs += [(kind, 0, t) for kind in ("tr", "gram") for t in range(TC)]
    act = [j for j in jobs if j[0] not in ("stat0", "stat1", "gram")]
    return {j: i for i, j in enumerate(jobs)}, {j: i for i, j in enumerate(act)}


PLAN = {last: plan(last) for last in (False, True)}
JOBS, ACTS = len(PLAN[False][0]), len(PLAN[False][1])
FIRST_JOBS, FIRST_ACTS = 2 * TC, TC
STEPS = HEADS * NT
ATT = N * STEPS
RING = 3
AHEAD = 12
PRIME = 4
SQUARINGS = 3
ROUNDS = 8
GROUP = 4
PER_ROUND_DVE = 2 * SQUARINGS + 2
PER_ROUND_PE = 4 * SQUARINGS + 1
DVE_SETUP_CHAIN = 39
DVE_IMAGE_CHAIN = 88
DVE_ROUND_CHAIN = 2


def spread(ap, dim, n):
    ap = ap.unsqueeze(dim)
    return ap.broadcast_to([n if i == dim else k for i, k in enumerate(ap.shape)])


def build(nc, x, w_all, bn, r_in, sel_in, consts, l1w, l1b, out):
    x1d = nc.dram_tensor("x1_scratch", (B, TC, P, HW), F32).ap()
    x_v = x.rearrange("b (t p) h w -> b t p (h w)", p=P)
    out_v = out.rearrange("b (t p) h w -> b t p (h w)", p=P)
    ctx = ExitStack()
    with ctx:
        def sb(name, shape, dt):
            return ctx.enter_context(nc.sbuf_tensor(name, shape, dt))

        def sem(name):
            return ctx.enter_context(nc.semaphore(name))

        WH = sb("w_hi", [P, W_END], F16)
        WL = sb("w_lo", [P, W_END], F16)
        X = sb("x_tiles", [P, TC, HW], F32)
        Y0 = sb("y0", [P, 2, TH, HW], F16)
        YP = sb("y_padded", [P, N + 1, 2, TH, PF, PF], F16)
        Z = sb("z", [P, 2, TH, HW], F16)
        SH = sb("shared", [P, TC, 2, HW], F16)
        QK3 = sb("q3_k2", [P, 2, HEADS, HW], F16)
        V = sb("v", [P, NT, HEADS, VW + 1], F16)
        R4 = sb("ring", [P, 4, HW], F32)
        AO = sb("attn_out", [P, NT, CH], F32)
        CST = sb("consts", [P, 4, P], F32)
        BNS = sb("bn_scale", [P, NBN], F32)
        BNB = sb("bn_bias", [P, NBN], F32)
        RHL = sb("positions", [P, N, TH, P], F16)
        SEL = sb("select", [P, HW], F16)
        LW = sb("l1_w", [P, TC], F32)
        LB = sb("l1_b", [P, TC], F32)
        HALFNEG = sb("minus_half", [P, NBN], F32)
        SHIFT = sb("shift", [P, 1], F32)
        BST = sb("bn_stats", [P, TC, 2, 6], F32)
        MV = sb("mean_var", [P, TC, 2], F32)
        ST = sb("mean_sq", [P, TC, 2], F32)
        GS = sb("group_mean_sq", [P, TC, 2], F32)
        VAR = sb("group_var", [P, TC], F32)
        RST = sb("rstd", [P, TC], F32)
        NB = sb("norm_bias", [P, TC], F32)
        NM = sb("minus_max", [P, HEADS * NT], F32)
        NMT = sb("minus_max_t", [NT, 2, P], F16)
        RC = sb("recip", [P, NT], F32)
        COV = sb("cov", [P, TC, P], F32)
        BNR = COV[:, 0, 0:4 * NBN].rearrange("p (k n) -> p k n", n=NBN)
        MU = sb("mu", [P, TC], F32)
        RSB = sb("rstd_of_images", [P, B + 1, TC], F32)
        NBB = sb("norm_bias_of_images", [P, B, TC], F32)

        ps = ctx.enter_context(nc.psum_tensor("ps", [P, 8, HALF], F32))

        def pair(j):
            return ps[:, 2 * (j % 4):2 * (j % 4) + 2, :].rearrange("p a n -> p (a n)")

        ident, avg16, ones64, ones = (CST[:, i, :] for i in range(4))
        XNH = AO[:, :, :].rearrange("p a c -> p (a c)").bitcast(F16).rearrange("p (t n) -> p t n", t=TC)
        XNL = Z[:, :, :, :].rearrange("p s t n -> p (s t) n")
        Q2 = SH[:, :, 0, :]
        K1 = SH[:, :, 1, :]
        Q3 = QK3[:, 0, :, :]
        K2 = QK3[:, 1, :, :]
        X1 = SH[:, :, :, :].rearrange("p t s n -> p t (s n)").bitcast(F32)
        YT = QK3[:, :, :, :].rearrange("p q (h g) n -> p (q h) (g n)", g=2).bitcast(F32)\
            .rearrange("p t (a c) -> p t a c", c=P)
        STAGE = X1
        U = R4[:, 0:2, :]
        T = R4[:, 2:4, :]
        PF32 = R4[:, 0:RING, :]
        Z32 = Z[:, :, :, :].rearrange("p s t n -> p (s t n)").bitcast(F32).rearrange("p (r n) -> p r n", n=HW)
        PHL = [m.bitcast(F16).rearrange("p (s n) -> p s n", s=2) for m in (R4[:, RING, :], Z32[:, 0, :], Z32[:, 1, :])]

        def w2(Wt, base, k, width, lo, n):
            return Wt[:, base + k * width + lo:base + k * width + lo + n]

        wloaded = [sem(f"weights_loaded{i}") for i in range(4)]
        whigh = sem("weights_hi")
        wsplit = sem("weights_split")
        small_loaded = sem("small_loaded")
        setup_pool = sem("setup_pool")
        setup_dve = sem("setup_done")
        x_loaded = [sem(f"x_loaded{i}") for i in range(TC)]
        xn_ready = sem("xn_ready")
        xres_loaded = [sem(f"x_again{i}") for i in range(TC)]
        x1_stored = [sem(f"x1_stored{i}") for i in range(TC)]
        job_done = sem("job_done")
        act_done = sem("act_done")
        drained = sem("drained")
        stat_ready = sem("stat_ready")
        var_ready = sem("var_ready")
        rstd_ready = sem("rstd_ready")
        mx_done = sem("max_logits_done")
        mx_used = sem("max_taken")
        nmt_done = sem("max_transposed")
        nmt_ready = sem("max_row_ready")
        aug_loaded = sem("max_row_placed")
        qk_done = sem("logits_done")
        exp_done = sem("exp_done")
        ph_done = sem("p_hi_done")
        pl_done = sem("p_lo_done")
        pv_done = sem("pv_done")
        o_used = sem("head_output_taken")
        chain = sem("dve_chain")
        l1_loaded = [sem(f"x1_loaded{i}") for i in range(GROUP * TC)]
        l1_stored = [sem(f"out_stored{i}") for i in range(4)]
        fin_pe = sem("fin_pe")
        fin_dve = sem("fin_dve")
        fin_stage = sem("fin_stage")
        fin_pool = sem("fin_pool")
        ap_done = sem("applied")
        ap_used = sem("applied_taken")
        mat_ready = sem("matrices_ready")
        fin_act = sem("fin_act")
        bn_read = sem("bn_loaded")
        bn_rstd = sem("bn_rstd")
        bn_ready = sem("bn_ready")

        block = ctx.enter_context(nc.Block())

        L1 = R4[:, :, :].rearrange("p r (t c) -> p r t c", t=8)
        BC = AO[:, :, :].rearrange("p a c -> p (a c)").rearrange("p (i t c) -> p i t c", i=4, t=4)
        Zf = Z[:, :, :, :].rearrange("p s t n -> p (s t n)").bitcast(F32).rearrange("p (i t c) -> p i t c", i=4, t=4)
        V4 = Y0[:, :, :, :].rearrange("p s t n -> p (s t n)").bitcast(F32)
        A_, Bm, Cm, W_ = (BC[:, i, :, :] for i in range(4))
        NY, NZ, NTm, SUB = (Zf[:, i, :, :] for i in range(4))
        SCR = L1[:, 0, 0:TC, :]
        SCR2 = L1[:, 1, 0:TC, :]
        I15 = L1[:, 2, 0, :]
        TR = V4[:, P:P + 8]
        IV = V4[:, P + 8:P + 16]
        DG = V4[:, P + 16:P + 24]
        EV = V4[:, P + 24:P + 40]
        CB = V4[:, P + 64:P + 64 + TC * B].rearrange("p (t b) -> p t b", t=TC)
        MB = V4[:, P + 128:P + 128 + TC * B].rearrange("p (t b) -> p t b", t=TC)
        LIN_H = WH[:, 0:8 * 2 * HW].bitcast(F32).rearrange("p (t n) -> p t n", n=HW)
        LIN_L = WL[:, 0:8 * 2 * HW].bitcast(F32).rearrange("p (t n) -> p t n", n=HW)

        def lin(i, t):
            return (LIN_H if i < GROUP // 2 else LIN_L)[:, (i % (GROUP // 2)) * TC + t, :]
        LOUT = X[:, :, :]
        SB = WH[:, 8 * 2 * HW:8 * 2 * HW + TC * 2 * P].bitcast(F32).rearrange("p (r c) -> p r c", c=P)

        def tiles(m):
            return m.rearrange("p (t c) -> p t c", c=P)

        def fin_pe_part(pe, mm):
            def blocks(dst, lhs, rhs):
                for t in range(TC):
                    ins = mm(dst[:, t * P:(t + 1) * P], lhs(t), rhs[:, t, :], start=True, stop=True)
                return ins

            def of(m):
                return lambda t: m[:, t, :]

            def all_ones(t):
                return ones
            pe.wait_ge(fin_stage, 1)
            blocks(pair(0), all_ones, SCR).then_inc(fin_pe, 1)
            pe.wait_ge(fin_stage, 2)
            mm(pair(1)[:, 0:TC], ones64, DG[:, 0:TC], start=True, stop=True).then_inc(fin_pe, 1)
            pe.wait_ge(fin_stage, 3)
            with pe.Fori(0, ROUNDS) as r:
                for k in range(SQUARINGS):
                    base = 3 + r * PER_ROUND_DVE + k * 2
                    pe.wait_ge(fin_stage, base)
                    pe.wait_ge(fin_act, 1 + r * 2 * SQUARINGS + 2 * k)
                    blocks(pair(1), of(NZ), NY).then_inc(fin_pe, 1)
                    blocks(pair(0), of(Bm), Bm).then_inc(fin_pe, 1)
                    blocks(pair(3), of(Cm), Cm).then_inc(fin_pe, 1)
                    pe.wait_ge(fin_stage, base + 1)
                    blocks(pair(2)[:, HALF:], of(NTm), NZ)
                    blocks(pair(1)[:, HALF:], of(NY), NTm).then_inc(fin_pe, 1)
                pe.wait_ge(fin_stage, 3 + r * PER_ROUND_DVE + 2 * SQUARINGS + 1)
                mm(pair(3)[:, 0:8], ones64, DG[:, 0:8], start=True, stop=True).then_inc(fin_pe, 1)
            last = 3 + ROUNDS * PER_ROUND_DVE
            pe.wait_ge(fin_stage, last + 1)
            mm(pair(3)[:, 0:8], ones64, DG[:, 0:8], start=True, stop=True).then_inc(fin_pe, 1)
            pe.wait_ge(fin_stage, last + 2)
            blocks(pair(0), all_ones, SCR).then_inc(fin_pe, 1)
            pe.wait_ge(fin_stage, last + 3)
            for t in range(TC):
                ins = mm(pair(1)[:, t * B:(t + 1) * B], SUB[:, t, :], MB[:, t, :], start=True, stop=True)
            ins.then_inc(fin_pe, 1)

        def count_drained(b, j, last):
            return b * JOBS + (PRIME + FIRST_JOBS + PLAN[last][0][j] + 1)

        def count_done(b, j, last):
            return b * JOBS + (FIRST_JOBS + PLAN[last][0][j] + 1)

        def count_act(b, j, last):
            return b * ACTS + (FIRST_ACTS + PLAN[last][1][j] + 1)

        def count_stat(b, which, t, last):
            return b * 2 * TC + TC + (0 if last or which == 0 else TC) + t + 1

        def bank_pair(j, last=False):
            return pair(PLAN[last][0][j])

        @block.sync
        def _(sp):
            for dst, src in ((CST[:, :, :], consts), (BNR[:, :, :], bn), (R4[:, 0, 0:HALF], r_in),
                             (SEL[:, :], sel_in), (LW[:, :], l1w), (LB[:, :], l1b)):
                sp.dma_start(dst, src).then_inc(small_loaded, 16)
            for t in range(TC):
                sp.dma_start(X[:, t, :], x_v[0, t, :, :]).then_inc(x_loaded[t], 16)
            for c in range(WCHUNKS):
                if c >= 4:
                    sp.wait_ge(wsplit, c - 3)
                sp.dma_start(STAGE[:, c % 4, :], w_all[:, c * WCHUNK:(c + 1) * WCHUNK]).then_inc(wloaded[c % 4], 16)

            def image(b, last, following=None):
                if not last:
                    sp.wait_ge(xn_ready, following * TC)
                    for t in range(TC):
                        sp.dma_start(X[:, t, :], x_v[following, t, :, :]).then_inc(x_loaded[t], 16)
                for n in range(N):
                    for h in range(HEADS):
                        sp.wait_ge(nmt_ready, (b * N + n) * HEADS + h + 1)
                        sp.dma_start(Q3[HD:HD + 1, h, :], NMT[:, h % 2, :]).then_inc(aug_loaded, 16)
                sp.wait_ge(pv_done, b * ATT + ATT + RING)
                for t in range(TC):
                    sp.dma_start(X1[:, t, :], x_v[b, t, :, :]).then_inc(xres_loaded[t], 16)
                for t in range(TC):
                    sp.wait_ge(drained, count_drained(b, ("cv2", 0, t), last))
                    sp.dma_start(x1d[b, t, :, :], X1[:, t, :]).then_inc(x1_stored[t], 16)

            with sp.Fori(1, B) as following:
                image(following - 1, False, following)
            image(B - 1, True)
            for t in range(TC):
                sp.wait_ge(x1_stored[t], 16 * B)
            with sp.Fori(0, B // GROUP) as g:
                for i in range(GROUP):
                    for t in range(TC):
                        sp.wait_ge(ap_used, g * GROUP * TC + i * TC + t + 1)
                        sp.dma_start(lin(i, t), x1d[g * GROUP + i, t, :, :]).then_inc(l1_loaded[i * TC + t], 16)
            for t in range(TC):
                sp.wait_ge(l1_stored[t], 16 * B + 16)

        @block.gpsimd
        def _(pool):
            g = nc.gpsimd
            g.memset(YP[:, :, :, :, :, :], 0.0).then_inc(setup_pool, 1)
            pool.wait_ge(setup_pool, 1)
            g.memset(K2[HD:HD + 1, :, :], MSCALE).then_inc(setup_pool, 1)
            pool.wait_ge(setup_pool, 2)
            g.memset(V[:, :, :, :], 1.0).then_inc(setup_pool, 1)
            pool.wait_ge(bn_read, 1)
            g.tensor_tensor(BNS[:, :], BNR[:, 3, :], HALFNEG[:, :], ALU.pow).then_inc(bn_rstd, 1)

            def rstds(count):
                for t in range(TC):
                    pool.wait_ge(var_ready, count(t))
                    g.tensor_tensor(RST[:, t:t + 1], VAR[:, t:t + 1], HALFNEG[:, 0:1], ALU.pow).then_inc(rstd_ready, 1)

            def image(b, last):
                for n in range(N):
                    if n == 1 and not last:
                        rstds(lambda t: count_stat(b, 0, t, last))
                    for s in range(STEPS):
                        pool.wait_ge(ph_done, b * ATT + n * STEPS + s + 1)
                        g.tensor_tensor(PHL[s % RING][:, 1, :], PF32[:, s % RING, :], PHL[s % RING][:, 0, :], ALU.subtract)\
                            .then_inc(pl_done, 1)
                rstds(lambda t: count_stat(b, 1, t, last))

            rstds(lambda t: t + 1)
            with pool.Fori(0, B - 1) as b:
                image(b, False)
            image(B - 1, True)
            pool.wait_ge(fin_dve, 1)
            g.tensor_tensor(EV[:, 8:16], EV[:, 0:8], HALFNEG[:, 0:8], ALU.pow).then_inc(fin_pool, 1)

        @block.scalar
        def _(act):
            a = nc.scalar
            for c in range(WCHUNKS):
                act.wait_ge(wloaded[c % 4], 16 * (c // 4 + 1))
                a.activation(WH[:, c * WCHUNK:(c + 1) * WCHUNK], STAGE[:, c % 4, :], ACT.Copy, scale=WSCALE)\
                    .then_inc(whigh, 1)

            def silu_of(i, done, free, col):
                act.wait_ge(job_done, done)
                act.wait_ge(drained, free)
                a.activation(U[:, i % 2, :], pair(i), ACT.Identity, bias=BNB[:, col:col + 1], scale=BNS[:, col:col + 1])
                a.activation(T[:, i % 2, :], pair(i), ACT.Tanh, bias=BNB[:, col:col + 1],
                             scale=BNS[:, col:col + 1]).then_inc(act_done, 1)

            def image(b, last):
                def silu_part(j, col):
                    silu_of(PLAN[last][0][j], count_done(b, j, last), count_drained(b, j, last) - 2, col)

                def turned_max(n, h):
                    act.wait_ge(nmt_done, (b * N + n) * HEADS + h + 1)
                    a.activation(NMT[:, h % 2, :], ps[0:NT, 4 if h else 0, 0:P], ACT.Copy, scale=1.0 / MSCALE)\
                        .then_inc(nmt_ready, 1)

                for n in range(N):
                    for t in range(TH):
                        silu_part(("conv", n, t), BN_M + n * TH + t)
                    for kind, dst in (("q", Q2), ("k", K1)):
                        for t in range(TH):
                            j = (kind, n, t)
                            act.wait_ge(job_done, count_done(b, j, last))
                            for e in range(2):
                                r = slice(e * HD, (e + 1) * HD)
                                ins = a.activation(dst[r, 2 * t + e, :], bank_pair(j, last)[r, :], ACT.Copy,
                                                   scale=1.0 / WSCALE)
                            ins.then_inc(act_done, 1)
                    turned_max(n, 0)
                    for t in range(2):
                        j = ("v", n, t)
                        act.wait_ge(job_done, count_done(b, j, last))
                        a.activation(V[:, 4 * t:4 * t + 4, :, 0:HD],
                                     bank_pair(j, last).rearrange("p (i h d) -> p i h d", i=4, h=HEADS), ACT.Copy,
                                     scale=1.0 / WSCALE).then_inc(act_done, 1)
                    for s in range(STEPS):
                        act.wait_ge(qk_done, b * ATT + n * STEPS + s + 1)
                        act.wait_ge(pl_done, b * ATT + n * STEPS + s + 1)
                        a.activation(PF32[:, s % RING, :], pair(s % 2), ACT.Exp, bias=SHIFT[:, 0:1],
                                     scale=HD ** -0.5).then_inc(exp_done, 1)
                        if s % NT == 4 and s + NT < STEPS:
                            turned_max(n, s // NT + 1)
                    for t in range(TH):
                        j = ("aot", n, t)
                        act.wait_ge(job_done, count_done(b, j, last))
                        a.activation(Z[:, 0, t, :], bank_pair(j, last), ACT.Copy).then_inc(act_done, 1)
                    for t in range(TH):
                        silu_part(("proj", n, t), BN_PROJ + n * TH + t)
                for t in range(TC):
                    silu_part(("cv2", 0, t), BN_CV2 + t)
                if not last:
                    for t in range(TC):
                        silu_part(("cv1", 0, t), BN_CV1 + t)
                for t in range(TC):
                    j = ("tr", 0, t)
                    act.wait_ge(job_done, count_done(b, j, last))
                    a.activation(YT[:, t, 0:NT // 2, :].rearrange("p a c -> p (a c)"),
                                 bank_pair(j, last)[:, 0:HALF], ACT.Copy).then_inc(act_done, 1)

            act.wait_ge(bn_ready, 1)
            for t in range(TC):
                silu_of(TC + t, TC + t + 1, PRIME + TC + t - 1, BN_CV1 + t)
            with act.Fori(0, B - 1) as b:
                image(b, False)
            image(B - 1, True)

            with act.Fori(0, ROUNDS) as r:
                for k in range(SQUARINGS):
                    done = 2 + r * PER_ROUND_PE + 4 * k
                    act.wait_ge(fin_pe, done + 2)
                    a.activation(Bm, tiles(pair(0)[:, 0:HALF]), ACT.Copy)
                    act.wait_ge(fin_pe, done + 3)
                    a.activation(Cm, tiles(pair(3)[:, 0:HALF]), ACT.Copy).then_inc(fin_act, 1)
                    act.wait_ge(fin_pe, done + 4)
                    a.activation(NZ, tiles(pair(2)[:, HALF:]), ACT.Copy).then_inc(fin_act, 1)
            with act.Fori(0, B) as b:
                for t in range(TC):
                    act.wait_ge(ap_used, b * TC + t + 1 + GROUP * TC)
                    act.dma_start(out_v[b, t, :, :], LOUT[:, t, :]).then_inc(l1_stored[t], 16)

        @block.tensor
        def _(pe):
            mm = nc.tensor.matmul

            def products(o, parts, rhs_of):
                last = len(parts) - 1
                for i, (w, key) in enumerate(parts):
                    for h in range(2):
                        ins = mm(o[:, h * HALF:(h + 1) * HALF], w, rhs_of(key, h), start=(i == 0), stop=(i == last))
                ins.then_inc(job_done, 1)

            def three(w_hi, w_lo, key):
                return [(w_hi, (0, key)), (w_hi, (1, key)), (w_lo, (0, key))]

            def cv1(o, t):
                parts = []
                for k in range(TC):
                    parts += three(w2(WH, W_CV1, k, C, t * P, P), w2(WL, W_CV1, k, C, t * P, P), k)
                products(o, parts, lambda key, h: (XNH, XNL)[key[0]][:, key[1], h * HALF:(h + 1) * HALF])

            def zr(key, h):
                return Z[:, key[0], key[1], h * HALF:(h + 1) * HALF]

            def module(b, n, last):
                def begin(j):
                    pe.wait_ge(drained, count_drained(b, j, last) - 4)

                pe.wait_ge(drained, count_drained(b, ("conv", n, 0), last) - 1)
                for t in range(TH):
                    begin(("conv", n, t))
                    parts = []
                    for k in range(TH):
                        for tap in range(TAPS):
                            base = W_M + (n * TAPS + tap) * TH * CH
                            parts += three(w2(WH, base, k, CH, t * P, P), w2(WL, base, k, CH, t * P, P), (k, tap))

                    def shifted(key, h):
                        hl, (k, tap) = key
                        y0, dx = tap // 3 + h * (F // 2), tap % 3
                        return YP[:, n, hl, k, y0:y0 + F // 2, dx:dx + F]
                    products(bank_pair(("conv", n, t), last), parts, shifted)
                if n == 1 and not last:
                    for t in range(TC):
                        begin(("stat0", 0, t))
                        pe.wait_ge(stat_ready, count_stat(b, 0, t, last))
                        mm(bank_pair(("stat0", 0, t))[:, 0:2], avg16, ST[:, t, :], start=True, stop=True)\
                            .then_inc(job_done, 1)
                pe.wait_ge(drained, count_drained(b, ("conv", n, 1), last))
                wq = W_QKV + n * TH * 3 * CH
                for m in range(2 * TH):
                    j = ("qk"[m // TH], n, m % TH)
                    begin(j)
                    parts = []
                    for k in range(TH):
                        parts += three(w2(WH, wq, k, 3 * CH, m * P, P), w2(WL, wq, k, 3 * CH, m * P, P), k)
                    if m >= TH:
                        parts.append((RHL[:, n, m - TH, :], None))
                    products(bank_pair(j, last), parts,
                             lambda key, h: SEL[:, h * HALF:(h + 1) * HALF] if key is None else zr(key, h))
                pe.wait_ge(drained, count_drained(b, ("k", n, 1), last))

                def max_logits(m, o):
                    h, i = m // NT, m % NT
                    for e in range(2):
                        ins = mm(o[:, e * HALF:(e + 1) * HALF], Q2[:, h, i * P:(i + 1) * P],
                                 K1[:, h, e * HALF:(e + 1) * HALF], start=True, stop=True)
                    ins.then_inc(mx_done, 1)

                def turn_max(h, bank):
                    nc.tensor.transpose(ps[0:NT, bank, 0:P], NM[:, h * NT:(h + 1) * NT], ident).then_inc(nmt_done, 1)

                for m in range(AHEAD):
                    if m >= 4:
                        pe.wait_ge(mx_used, b * ATT + n * STEPS + m - 3)
                    max_logits(m, pair(m))
                pe.wait_ge(mx_used, b * ATT + n * STEPS + AHEAD)
                turn_max(0, 0)
                for t in range(2):
                    begin(("v", n, t))
                    for i in range(4):
                        pos = (4 * t + i) * P
                        o = bank_pair(("v", n, t), last)[:, i * CH:(i + 1) * CH]
                        for k in range(TH):
                            zh, zl = Z[:, 0, k, pos:pos + P], Z[:, 1, k, pos:pos + P]
                            vh, vl = w2(WH, wq, k, 3 * CH, 2 * CH, CH), w2(WL, wq, k, 3 * CH, 2 * CH, CH)
                            mm(o, zh, vh, start=(k == 0), stop=False)
                            mm(o, zh, vl, start=False, stop=False)
                            ins = mm(o, zl, vh, start=False, stop=(k == TH - 1))
                    ins.then_inc(job_done, 1)

                def logits(s):
                    h, i = s // NT, s % NT
                    keys = slice(i * P, (i + 1) * P)
                    if i == 0:
                        pe.wait_ge(aug_loaded, ((b * N + n) * HEADS + h + 1) * 16)
                    if s >= 2:
                        pe.wait_ge(exp_done, b * ATT + n * STEPS + s - 1)
                    o = pair(s % 2)
                    for e in range(2):
                        mm(o[:, e * HALF:(e + 1) * HALF], K1[:, h, keys], Q2[:, h, e * HALF:(e + 1) * HALF],
                           start=True, stop=False)
                    for e in range(2):
                        ins = mm(o[:, e * HALF:(e + 1) * HALF], K2[0:HD + 1, h, keys],
                                 Q3[0:HD + 1, h, e * HALF:(e + 1) * HALF], start=False, stop=True)
                    ins.then_inc(qk_done, 1)

                def values(s):
                    h, i = s // NT, s % NT
                    pe.wait_ge(pl_done, b * ATT + n * STEPS + s + 1 + RING)
                    if i == 0:
                        pe.wait_ge(o_used, (b * N + n) * HEADS + h + 1)
                    vh1, vl, done = V[:, i, h, 0:HD + 1], V[:, i, h, HD + 1:VW], i == NT - 1
                    for q in range(NT):
                        o = ps[:, 6 + q // 4, (q % 4) * P:(q % 4) * P + HD + 1]
                        ph = PHL[s % RING][:, 0, q * P:(q + 1) * P]
                        pl = PHL[s % RING][:, 1, q * P:(q + 1) * P]
                        mm(o, ph, vh1, start=(i == 0 and q % 4 == 0), stop=False, skip_group_check=True)
                        mm(o[:, 0:HD], ph, vl, start=False, stop=False, skip_group_check=True)
                        ins = mm(o, pl, vh1, start=False, stop=done, skip_group_check=True)
                    ins.then_inc(pv_done, 1)

                logits(0)
                logits(1)
                pe.wait_ge(drained, count_drained(b, ("v", n, 1), last))
                for s in range(STEPS):
                    if s + 2 < STEPS:
                        logits(s + 2)
                    if s + AHEAD <= STEPS:
                        pe.wait_ge(mx_used, b * ATT + n * STEPS + s + AHEAD)
                    if s % NT == 4 and s + NT < STEPS:
                        h = s // NT + 1
                        turn_max(h, 4)
                        if s + AHEAD < STEPS:
                            pe.wait_ge(nmt_ready, (b * N + n) * HEADS + h + 1)
                    if s + AHEAD < STEPS:
                        max_logits(s + AHEAD, pair(2))
                    if s:
                        values(s - 1)
                values(STEPS - 1)
                pe.wait_ge(o_used, (b * N + n + 1) * HEADS + 1)
                for t in range(TH):
                    for i in range(NT):
                        ins = nc.tensor.transpose(bank_pair(("aot", n, t), last)[:, i * P:(i + 1) * P],
                                                  AO[:, i, t * P:(t + 1) * P], ident)
                    ins.then_inc(job_done, 1)
                pe.wait_ge(drained, count_drained(b, ("aot", n, 1), last))
                wp = W_PROJ + n * TH * CH
                for t in range(TH):
                    begin(("proj", n, t))
                    parts = []
                    for k in range(TH):
                        parts += three(w2(WH, wp, k, CH, t * P, P), w2(WL, wp, k, CH, t * P, P), k)
                    products(bank_pair(("proj", n, t), last), parts, zr)

            def image(b, last):
                for n in range(N):
                    module(b, n, last)

                def begin(j):
                    pe.wait_ge(drained, count_drained(b, j, last) - 4)

                def joined(key, h):
                    hl, k = key
                    if k < TH:
                        return Y0[:, hl, k, h * HALF:(h + 1) * HALF]
                    y0 = 1 + h * (F // 2)
                    return YP[:, k // TH - 1, hl, k % TH, y0:y0 + F // 2, 1:1 + F]
                pe.wait_ge(drained, count_drained(b, ("proj", 1, 0), last))
                for t in range(TC):
                    begin(("cv2", 0, t))
                    parts = []
                    for k in range((2 + N) * TH):
                        parts += three(w2(WH, W_CV2, k, C, t * P, P), w2(WL, W_CV2, k, C, t * P, P), k)
                    if t == 0:
                        pe.wait_ge(drained, count_drained(b, ("proj", 1, 1), last))
                    products(bank_pair(("cv2", 0, t), last), parts, joined)

                def next_cv1(ts):
                    for t in ts:
                        begin(("cv1", 0, t))
                        cv1(bank_pair(("cv1", 0, t)), t)
                if not last:
                    pe.wait_ge(xn_ready, b * TC + 2 * TC)
                    next_cv1(range(2))
                for t in range(TC):
                    begin(("stat1", 0, t))
                    pe.wait_ge(stat_ready, count_stat(b, 1, t, last))
                    mm(bank_pair(("stat1", 0, t), last)[:, 0:2], avg16, ST[:, t, :], start=True, stop=True)\
                        .then_inc(job_done, 1)
                if not last:
                    next_cv1(range(2, TC))
                for t in range(TC):
                    begin(("tr", 0, t))
                    pe.wait_ge(drained, count_drained(b, ("stat1", 0, t), last))
                    for i in range(NT):
                        ins = nc.tensor.transpose(bank_pair(("tr", 0, t), last)[:, i * P:(i + 1) * P],
                                                  X1[:, t, i * P:(i + 1) * P], ident)
                    ins.then_inc(job_done, 1)
                for t in range(TC):
                    pe.wait_ge(drained, count_drained(b, ("tr", 0, t), last))
                    for i in range(NT):
                        ins = mm(bank_pair(("gram", 0, t), last)[:, 0:P], YT[:, t, i, :], YT[:, t, i, :],
                                 start=(i == 0), stop=(i == NT - 1))
                    ins.then_inc(job_done, 1)

            pe.wait_ge(bn_read, 1)
            for t in range(TC):
                pe.wait_ge(stat_ready, t + 1)
                mm(pair(t)[:, 0:2], avg16, ST[:, t, :], start=True, stop=True).then_inc(job_done, 1)
            pe.wait_ge(xn_ready, TC)
            pe.wait_ge(wsplit, TC * C // WCHUNK)
            for t in range(TC):
                pe.wait_ge(drained, PRIME + t + 1)
                cv1(pair(TC + t), t)
            pe.wait_ge(setup_dve, 1)
            with pe.Fori(0, B - 1) as b:
                image(b, False)
            image(B - 1, True)

            fin_pe_part(pe, mm)
            with pe.Fori(0, B // GROUP) as g:
                for i in range(GROUP):
                    for t in range(TC):
                        pe.wait_ge(l1_loaded[i * TC + t], 16 * g + 16)
                        pe.wait_ge(mat_ready, g * GROUP * TC + i * TC + t + 1)
                        for h in range(2):
                            ins = mm(pair(t)[:, h * HALF:(h + 1) * HALF], SB[:, t, :],
                                     lin(i, t)[:, h * HALF:(h + 1) * HALF], start=True, stop=True)
                        ins.then_inc(ap_done, 1)

        @block.vector
        def _(dve):
            v = nc.vector

            class Own:
                base, n = 0, 0

                def mark(self, ins):
                    ins.then_inc(chain, 1)
                    self.n += 1

                def wait(self):
                    dve.wait_ge(chain, self.base + self.n)

                def __call__(self, ins):
                    self.mark(ins)
                    self.wait()
            own = Own()

            def drain(ins):
                ins.then_inc(drained, 1)

            def split(hi, lo, src):
                own(v.tensor_copy(hi, src))
                return v.tensor_tensor(lo, src, hi, ALU.subtract)

            def stats(src, t):
                v.bn_stats(BST[:, t, 0, :], src[:, t, 0:HALF])
                return v.bn_stats(BST[:, t, 1, :], src[:, t, HALF:])

            def joined_stats(t):
                return v.bn_aggr(MV[:, t, :], BST[:, t, :, :].rearrange("p a s -> p (a s)"))

            def mean_and_square(t):
                v.tensor_copy(ST[:, t, 0:1], MV[:, t, 0:1])
                v.scalar_tensor_tensor(ST[:, t, 1:2], MV[:, t, 0:1], MV[:, t, 0:1], MV[:, t, 1:2], ALU.mult,
                                       ALU.add).then_inc(stat_ready, 1)

            def image_stats(count):
                for t in range(3):
                    dve.wait_ge(x_loaded[t], count)
                    own.mark(stats(X, t))
                dve.wait_ge(x_loaded[3], count)
                own.wait()
                own.mark(stats(X, 3))
                for t in range(3):
                    joined_stats(t)
                own(v.memset(NB[:, 0:1], 0.0))
                for t in range(3):
                    mean_and_square(t)
                own(joined_stats(3))
                mean_and_square(3)

            def variances(bank, count):
                for t in range(TC):
                    dve.wait_ge(job_done, count(t))
                    own(v.tensor_copy(GS[:, t, :], bank(t)[:, 0:2]))
                    own(v.scalar_tensor_tensor(VAR[:, t:t + 1], GS[:, t, 0:1], GS[:, t, 0:1], GS[:, t, 1:2],
                                               ALU.mult, ALU.subtract))
                    v.tensor_scalar(VAR[:, t:t + 1], VAR[:, t:t + 1], -1.0, GN_EPS, ALU.mult, ALU.add)\
                        .then_inc(var_ready, 1)

            def norm_bias(t, count):
                dve.wait_ge(rstd_ready, count)
                return v.scalar_tensor_tensor(NB[:, t:t + 1], GS[:, t, 0:1], -1.0, RST[:, t:t + 1], ALU.mult, ALU.mult)

            def normalised(src, t):
                return v.tensor_scalar(src[:, t, :], src[:, t, :], RST[:, t:t + 1], NB[:, t:t + 1], ALU.mult, ALU.add)

            def normalise_image():
                for t in range(TC):
                    own(normalised(X, t))
                    split(XNH[:, t, :], XNL[:, t, :], X[:, t, :]).then_inc(xn_ready, 1)

            def silu(i, count):
                dve.wait_ge(act_done, count)
                u = U[:, i % 2, :]
                own(v.scalar_tensor_tensor(u, T[:, i % 2, :], 1.0, u, ALU.add, ALU.mult))
                return u

            def padded(n, hl, t):
                return YP[:, n, hl, t, 1:1 + F, 1:1 + F]

            def square(m):
                return m.rearrange("p (y x) -> p y x", x=F)

            def cv1_out(t, u):
                if t < TH:
                    drain(split(Y0[:, 0, t, :], Y0[:, 1, t, :], u))
                else:
                    drain(split(padded(0, 0, t - TH), padded(0, 1, t - TH), square(u)))

            v.memset(RC[:, 0:1], 0.0).then_inc(drained, PRIME)
            v.memset(RC[:, 1:2], 0.0).then_inc(pl_done, RING)
            v.memset(RC[:, 2:3], 0.0).then_inc(pv_done, RING)
            v.memset(RC[:, 3:4], 0.0).then_inc(o_used, 1)
            v.memset(RC[:, 4:5], 0.0).then_inc(fin_act, 1)
            v.memset(SHIFT[:, :], PSHIFT)
            v.memset(RSB[:, :, :], 0.0)
            v.memset(MU[:, :], 0.0)
            v.memset(HALFNEG[:, :], -0.5)
            dve.wait_ge(small_loaded, 6 * 16)
            v.tensor_scalar(BNR[:, 3, :], BNR[:, 3, :], BN_EPS, None, ALU.add).then_inc(bn_read, 1)
            image_stats(16)
            raw = R4[:, 0, 0:HALF].rearrange("p (n t c) -> p n t c", n=N, t=TH)
            own(v.tensor_scalar(RHL[:, :, :, :], raw, WSCALE, None, ALU.mult))
            own(v.scalar_tensor_tensor(RHL[HD:P, :, :, :], raw[HD:P, :, :, :], WSCALE, RHL[HD:P, :, :, :], ALU.mult,
                                       ALU.subtract))
            dve.wait_ge(bn_rstd, 1)
            own(v.tensor_tensor(BNS[:, :], BNS[:, :], BNR[:, 0, :], ALU.mult))
            own(v.tensor_tensor(BNB[:, :], BNR[:, 2, :], BNS[:, :], ALU.mult))
            own(v.tensor_tensor(BNB[:, :], BNR[:, 1, :], BNB[:, :], ALU.subtract))
            v.tensor_scalar(BNB[:, :], BNB[:, :], 0.5, None, ALU.mult)
            v.tensor_scalar(BNS[:, :], BNS[:, :], 0.5 / WSCALE, None, ALU.mult).then_inc(bn_ready, 1)
            v.memset(COV[:, :, :], 0.0)
            variances(lambda t: pair(t), lambda t: t + 1)
            for t in range(TC):
                own(norm_bias(t, t + 1))
                drain(v.memset(RC[:, 5:6], 0.0))
            normalise_image()
            for c in range(WCHUNKS):
                dve.wait_ge(whigh, c + 1)
                v.scalar_tensor_tensor(WL[:, c * WCHUNK:(c + 1) * WCHUNK], STAGE[:, c % 4, :], WSCALE,
                                       WH[:, c * WCHUNK:(c + 1) * WCHUNK], ALU.mult, ALU.subtract).then_inc(wsplit, 1)
            dve.wait_ge(setup_pool, 3)
            v.memset(NM[:, 0:1], 0.0).then_inc(setup_dve, 1)
            for t in range(TC):
                cv1_out(t, silu(TC + t, t + 1))
            assert own.n == DVE_SETUP_CHAIN, ("set-up", own.n)

            def image(b, last):
                def done(j):
                    dve.wait_ge(act_done, count_act(b, j, last))

                def silu_job(j):
                    return silu(PLAN[last][0][j], count_act(b, j, last))

                for n in range(N):
                    if n == 1 and not last:
                        image_stats(b * 16 + 32)
                    for t in range(TH):
                        drain(split(Z[:, 0, t, :], Z[:, 1, t, :], silu_job(("conv", n, t))))
                    if n == 1 and not last:
                        variances(lambda t: bank_pair(("stat0", 0, t)), lambda t: count_done(b, ("stat0", 0, t), last))
                        for t in range(TC):
                            drain(norm_bias(t, count_stat(b, 0, t, last)))
                    for t in range(TH):
                        j = ("q", n, t)
                        done(j)
                        for e in range(2):
                            r, o, h = slice(e * HD, (e + 1) * HD), slice((1 - e) * HD, (2 - e) * HD), 2 * t + e
                            v.tensor_copy(Q2[o, h, :], Q2[r, h, :])
                            ins = v.scalar_tensor_tensor(Q3[0:HD, h, :], bank_pair(j, last)[r, :], 1.0 / WSCALE,
                                                         Q2[r, h, :], ALU.mult, ALU.subtract)
                        drain(ins)
                    for t in range(TH):
                        j = ("k", n, t)
                        done(j)
                        for e in range(2):
                            r, o, h = slice(e * HD, (e + 1) * HD), slice((1 - e) * HD, (2 - e) * HD), 2 * t + e
                            v.tensor_copy(K2[0:HD, h, :], K1[r, h, :])
                            ins = v.scalar_tensor_tensor(K1[o, h, :], bank_pair(j, last)[r, :], 1.0 / WSCALE,
                                                         K1[r, h, :], ALU.mult, ALU.subtract)
                        drain(ins)

                    def take_max(m, o):
                        dve.wait_ge(mx_done, b * ATT + n * STEPS + m + 1)
                        v.tensor_reduce(NM[:, m:m + 1], o, AX.X, ALU.max, negate=True).then_inc(mx_used, 1)

                    for m in range(AHEAD):
                        take_max(m, pair(m))
                    for t in range(2):
                        j = ("v", n, t)
                        done(j)
                        drain(v.scalar_tensor_tensor(V[:, 4 * t:4 * t + 4, :, HD + 1:VW],
                                                     bank_pair(j, last).rearrange("p (i h d) -> p i h d", i=4, h=HEADS),
                                                     1.0 / WSCALE, V[:, 4 * t:4 * t + 4, :, 0:HD], ALU.mult,
                                                     ALU.subtract))

                    def head_output(h):
                        dve.wait_ge(pv_done, b * ATT + n * STEPS + (h + 1) * NT + RING)
                        o = ps[:, 6:8, :].rearrange("p a (q d) -> p (a q) d", d=P)
                        own(v.reciprocal(RC[:, :].unsqueeze(2), o[:, :, HD:HD + 1]))
                        v.tensor_tensor(AO[:, :, h * HD:(h + 1) * HD], o[:, :, 0:HD],
                                        spread(RC[:, :], 2, HD), ALU.mult).then_inc(o_used, 1)

                    for s in range(STEPS):
                        dve.wait_ge(exp_done, b * ATT + n * STEPS + s + 1)
                        dve.wait_ge(pv_done, b * ATT + n * STEPS + s + 1)
                        v.tensor_copy(PHL[s % RING][:, 0, :], PF32[:, s % RING, :]).then_inc(ph_done, 1)
                        if s % NT == 1 and s > 1:
                            head_output(s // NT - 1)
                        if s and s - 1 + AHEAD < STEPS:
                            take_max(s - 1 + AHEAD, pair(2))
                    head_output(HEADS - 1)
                    for t in range(TH):
                        done(("aot", n, t))
                        drain(v.tensor_tensor(Z[:, 1, t, :], bank_pair(("aot", n, t), last), Z[:, 0, t, :],
                                              ALU.subtract))
                    for t in range(TH):
                        u = square(silu_job(("proj", n, t)))
                        own(v.tensor_tensor(u, u, padded(n, 0, t), ALU.add))
                        own(v.tensor_tensor(u, u, padded(n, 1, t), ALU.add))
                        drain(split(padded(n + 1, 0, t), padded(n + 1, 1, t), u))
                if not last:
                    normalise_image()
                for t in range(TC):
                    u = silu_job(("cv2", 0, t))
                    dve.wait_ge(xres_loaded[t], b * 16 + 16)
                    drain(v.tensor_tensor(X1[:, t, :], X1[:, t, :], u, ALU.add))
                    own.wait()
                    dve.wait_ge(drained, count_drained(b, ("cv2", 0, t), last))
                    own.mark(stats(X1, t))
                for t in range(3):
                    joined_stats(t)
                own(v.memset(NB[:, 0:1], 0.0))
                for t in range(3):
                    mean_and_square(t)
                own(joined_stats(3))
                mean_and_square(3)
                if not last:
                    for t in range(2):
                        cv1_out(t, silu_job(("cv1", 0, t)))
                variances(lambda t: bank_pair(("stat1", 0, t), last), lambda t: count_done(b, ("stat1", 0, t), last))
                for t in range(TC):
                    own(norm_bias(t, count_stat(b, 1, t, last)))
                    v.tensor_copy(RSB[:, b, t:t + 1], RST[:, t:t + 1])
                    v.tensor_copy(NBB[:, b, t:t + 1], NB[:, t:t + 1])
                    own(v.tensor_scalar(MV[:, t, 0:1], MV[:, t, 0:1], RST[:, t:t + 1], NB[:, t:t + 1], ALU.mult,
                                        ALU.add))
                    v.tensor_tensor(MU[:, t:t + 1], MU[:, t:t + 1], MV[:, t, 0:1], ALU.add)
                    dve.wait_ge(x1_stored[t], b * 16 + 16)
                    drain(normalised(X1, t))
                if not last:
                    for t in range(2, TC):
                        cv1_out(t, silu_job(("cv1", 0, t)))
                for t in range(TC):
                    done(("tr", 0, t))
                    drain(v.tensor_copy(YT[:, t, NT // 2:, :].rearrange("p a c -> p (a c)"),
                                        bank_pair(("tr", 0, t), last)[:, HALF:]))
                for t in range(TC):
                    dve.wait_ge(job_done, count_done(b, ("gram", 0, t), last))
                    drain(v.tensor_tensor(COV[:, t, :], bank_pair(("gram", 0, t), last)[:, 0:P], COV[:, t, :], ALU.add))
                if not last:
                    v.memset(K2[HD:HD + 1, :, :], MSCALE)

            with dve.Fori(0, B - 1) as b:
                own.base, own.n = b * DVE_IMAGE_CHAIN + DVE_SETUP_CHAIN, 0
                image(b, False)
                assert own.n == DVE_IMAGE_CHAIN, ("image", own.n)
            own.base, own.n = DVE_SETUP_CHAIN + (B - 1) * DVE_IMAGE_CHAIN, 0
            image(B - 1, True)

            own(v.memset(TR[:, :], 0.0))
            for t in range(TC):
                v.memset(TR[:, TC + t:TC + t + 1], 0.0).then_inc(l1_stored[t], 16)
            v.memset(TR[:, 0:1], 0.0).then_inc(ap_used, GROUP * TC)
            own(v.tensor_scalar(MU[:, :], MU[:, :], 1.0 / B, None, ALU.mult))
            own(v.tensor_scalar(I15, ident, 1.5, None, ALU.mult))

            def stage(ins):
                ins.then_inc(fin_stage, 1)

            def along(s, n=P):
                return spread(s, 2, n)

            def each(m):
                return spread(m, 1, TC)

            stage(v.tensor_tensor(SCR, each(ident), along(MU[:, :]), ALU.mult))
            dve.wait_ge(fin_pe, 1)
            own(v.tensor_tensor(W_, tiles(pair(0)[:, 0:HALF]), along(MU[:, :]), ALU.mult))
            own(v.scalar_tensor_tensor(A_, COV[:, :, :], 1.0 / (B * HW), W_, ALU.mult, ALU.subtract))
            own(v.tensor_tensor(A_, A_, each(ones64), ALU.mult))
            own(v.scalar_tensor_tensor(A_, each(ident), COV_EPS, A_, ALU.mult, ALU.add))
            own(v.tensor_tensor(SCR, A_, each(ident), ALU.mult))
            stage(v.tensor_reduce(DG[:, 0:TC], SCR, AX.X, ALU.add))
            dve.wait_ge(fin_pe, 2)
            own(v.tensor_copy(TR[:, 0:TC], pair(1)[:, 0:TC]))
            own(v.reciprocal(IV[:, 0:TC], TR[:, 0:TC]))
            own(v.tensor_tensor(Bm, A_, along(IV[:, 0:TC]), ALU.mult))
            own(v.scalar_tensor_tensor(Cm, Bm, -1.0, each(ident), ALU.mult, ALU.add))
            v.tensor_scalar(Cm, Cm, 1.0 / 64, None, ALU.mult)
            v.tensor_copy(NY, Bm)
            stage(v.tensor_copy(NZ, each(ident)))

            fin_chain = own.base + own.n
            with dve.Fori(0, ROUNDS) as r:
                own.base, own.n = fin_chain + r * DVE_ROUND_CHAIN, 0
                for k in range(SQUARINGS):
                    done = 2 + r * PER_ROUND_PE + 4 * k
                    dve.wait_ge(fin_pe, done + 1)
                    stage(v.scalar_tensor_tensor(NTm, tiles(pair(1)[:, 0:HALF]), -0.5, each(I15), ALU.mult, ALU.add))
                    dve.wait_ge(fin_pe, done + 4)
                    stage(v.tensor_copy(NY, tiles(pair(1)[:, HALF:])))
                dve.wait_ge(fin_act, 1 + r * 2 * SQUARINGS + 2 * SQUARINGS - 1)
                v.tensor_tensor(SCR, Bm, each(ident), ALU.mult)
                own(v.tensor_tensor(SCR2, Cm, each(ident), ALU.mult))
                v.tensor_reduce(DG[:, 0:TC], SCR, AX.X, ALU.add)
                stage(v.tensor_reduce(DG[:, TC:2 * TC], SCR2, AX.X, ALU.add))
                dve.wait_ge(fin_pe, 2 + (r + 1) * PER_ROUND_PE)
                own(v.reciprocal(IV[:, :], pair(3)[:, 0:2 * TC]))
                v.tensor_tensor(Bm, Bm, along(IV[:, 0:TC]), ALU.mult)
                stage(v.tensor_tensor(Cm, Cm, along(IV[:, TC:]), ALU.mult))
                assert own.n == DVE_ROUND_CHAIN, ("round", own.n)
            own.base, own.n = fin_chain + ROUNDS * DVE_ROUND_CHAIN, 0
            own(v.memset(EV[:, 0:1], 0.0))
            dve.wait_ge(fin_act, 1 + ROUNDS * 2 * SQUARINGS)
            pe_done = 2 + ROUNDS * PER_ROUND_PE
            own(v.tensor_tensor(SCR, A_, Bm, ALU.mult))
            own(v.tensor_reduce(DG[:, 0:TC], SCR, AX.X, ALU.add))
            own(v.tensor_tensor(SCR, A_, Cm, ALU.mult))
            stage(v.tensor_reduce(DG[:, TC:2 * TC], SCR, AX.X, ALU.add))
            dve.wait_ge(fin_pe, pe_done + 1)
            own(v.tensor_scalar(IV[:, 0:TC], pair(3)[:, TC:2 * TC], COV_EPS, None, ALU.is_le))
            own(v.tensor_scalar(IV[:, TC:], IV[:, 0:TC], -1.0, 1.0, ALU.mult, ALU.add))
            v.tensor_copy(EV[:, TC:2 * TC], TR[:, 0:TC])
            v.tensor_copy(EV[:, 0:TC], pair(3)[:, 0:TC]).then_inc(fin_dve, 1)
            dve.wait_ge(fin_pool, 1)
            own(v.tensor_tensor(DG[:, 0:TC], EV[:, 2 * TC:3 * TC], IV[:, TC:], ALU.mult))
            own(v.tensor_tensor(DG[:, TC:2 * TC], EV[:, 3 * TC:], IV[:, 0:TC], ALU.mult))
            own(v.tensor_tensor(W_, Bm, along(DG[:, 0:TC]), ALU.mult))
            own(v.tensor_tensor(SUB, NZ, along(DG[:, TC:2 * TC]), ALU.mult))
            own(v.tensor_tensor(SUB, SUB, W_, ALU.add))
            stage(v.tensor_tensor(SCR, each(ident), along(LW[:, :]), ALU.mult))
            for t in range(TC):
                v.tensor_scalar(MB[:, t, :], NBB[:, :, t], -1.0, MU[:, t:t + 1], ALU.mult, ALU.add)
            dve.wait_ge(fin_pe, pe_done + 2)
            own(v.tensor_tensor(SUB, tiles(pair(0)[:, 0:HALF]), SUB, ALU.mult))
            stage(v.memset(EV[:, 0:1], 0.0))
            dve.wait_ge(fin_pe, pe_done + 3)
            for t in range(TC):
                ins = v.tensor_scalar(CB[:, t, :], pair(1)[:, t * B:(t + 1) * B], -1.0, LB[:, t:t + 1], ALU.mult,
                                      ALU.add)
            own(ins)
            for t in range(TC):
                v.tensor_scalar(SB[:, t, :], SUB[:, t, :], RSB[:, 0, t:t + 1], None, ALU.mult).then_inc(mat_ready, 1)
            with dve.Fori(0, B // GROUP) as g:
                for i in range(GROUP):
                    for t in range(TC):
                        dve.wait_ge(ap_done, g * GROUP * TC + i * TC + t + 1)
                        dve.wait_ge(l1_stored[t], g * GROUP * 16 + i * 16 + 16)
                        v.scalar_tensor_tensor(LOUT[:, t, :], pair(t), CB[:, t, bass.ds(g * GROUP + i, 1)], lin(i, t),
                                               ALU.add, ALU.add).then_inc(ap_used, 1)
                        v.tensor_scalar(SB[:, t, :], SUB[:, t, :], RSB[:, g * GROUP + i + 1, t:t + 1], None,
                                        ALU.mult).then_inc(mat_ready, 1)


_INS = ("x", "w_all", "bn", "r", "sel", "consts", "l1w", "l1b")


def kernel(x, L0_conv_cv1_w, L0_conv_cv1_bn, L0_conv_cv2_w, L0_conv_cv2_bn, L0_conv_m_cv1_w, L0_conv_m_cv1_bn,
           L0_conv_m_qkv_w, L0_conv_m_rw, L0_conv_m_rh, L0_conv_m_cv2_w, L0_conv_m_cv2_bn, L1_conv_weight,
           L1_conv_bias):
    import numpy as np
    import concourse.bacc as bacc
    from concourse.bass_utils import run_bass_kernel_spmd

    def turned(w):
        o, i = w.shape
        return w.reshape(o, i // P, P).transpose(2, 1, 0).reshape(P, -1)

    cv1, cv2, mc, qkv, mp = (np.asarray(a) for a in (L0_conv_cv1_w, L0_conv_cv2_w, L0_conv_m_cv1_w, L0_conv_m_qkv_w,
                                                     L0_conv_m_cv2_w))
    parts = [turned(cv1[:, :, 0, 0])]
    parts += [turned(mc[n, :, :, tap // 3, tap % 3]) for n in range(N) for tap in range(TAPS)]
    parts += [turned(qkv[n, :, :, 0, 0]) for n in range(N)]
    parts += [turned(mp[n, :, :, 0, 0]) for n in range(N)]
    parts += [turned(cv2[:, :, 0, 0])]
    w_all = np.ascontiguousarray(np.concatenate(parts, axis=1))
    bn1, bn2, bm, bp = (np.asarray(a) for a in (L0_conv_cv1_bn, L0_conv_cv2_bn, L0_conv_m_cv1_bn, L0_conv_m_cv2_bn))
    bn = np.concatenate([bn1, bm.transpose(1, 0, 2).reshape(4, -1), bp.transpose(1, 0, 2).reshape(4, -1), bn2], axis=1)
    bn = np.ascontiguousarray(bn.reshape(4, NBN, P).transpose(2, 0, 1))

    rw, rh = (np.asarray(r).reshape(N, TH, P, F).transpose(3, 0, 1, 2) for r in (L0_conv_m_rw, L0_conv_m_rh))
    r = np.concatenate([rw, rh, rw, rh], axis=0).reshape(P, -1)
    row, pos = np.arange(F)[:, None], np.arange(HW)[None]
    sel = np.concatenate([pos % F == row, pos // F == row] * 2, axis=0).astype(np.float16)
    i = np.arange(P)
    consts = np.stack([np.eye(P), (i[:, None] // 16 == i[None] // 16) / 16.0, i[:, None] // 64 == i[None] // 64,
                       np.ones((P, P))], axis=1).astype(np.float32)
    arrays = dict(x=np.ascontiguousarray(x), w_all=w_all, bn=bn, r=np.ascontiguousarray(r), sel=sel,
                  consts=np.ascontiguousarray(consts),
                  l1w=np.ascontiguousarray(np.asarray(L1_conv_weight).reshape(TC, P).T),
                  l1b=np.ascontiguousarray(np.asarray(L1_conv_bias).reshape(TC, P).T))
    nc = bacc.Bacc("TRN2", target_bir_lowering=False, num_devices=1)
    args = [nc.dram_tensor("in_" + k, arrays[k].shape, mybir.dt.from_np(arrays[k].dtype), kind="ExternalInput").ap() for k in _INS]
    out = nc.dram_tensor("out", (B, C, F, F), F32, kind="ExternalOutput").ap()
    build(nc, *args, out)
    ran = run_bass_kernel_spmd(nc, [{"in_" + k: arrays[k] for k in _INS}], core_ids=[0])
    return ran.results[0]["out"]
```

```python
from contextlib import ExitStack

import concourse.bass as bass
from concourse import mybir

F32 = mybir.dt.float32
F16 = mybir.dt.float16
ALU = mybir.AluOpType
ACT = mybir.ActivationFunctionType
AX = mybir.AxisListType

P = 128
B, C, F = 8, 512, 32
HW = F * F
CH = C // 2
N = 2
HEADS, HD = 4, 64
TC, TH = C // P, CH // P
PF = F + 2
TAPS = 9
NT = HW // P
HALF = 512
WSCALE = 64.0
BN_EPS, GN_EPS, COV_EPS = 1e-3, 1e-5, 1e-4
PSHIFT = 8 * 0.6931471805599453
MSCALE = 64.0
VW = 2 * HD + 1

W_CV1 = 0
W_M = W_CV1 + TC * C
W_QKV = W_M + N * TAPS * TH * CH
W_PROJ = W_QKV + N * TH * 3 * CH
W_CV2 = W_PROJ + N * TH * CH
W_END = W_CV2 + (2 + N) * TH * C
WCHUNK = 1024
WCHUNKS = W_END // WCHUNK
CONV_CHUNKS = -(-(W_M + TAPS * TH * CH) // WCHUNK)
WEIGHTS_AROUND_CV1 = [range(CONV_CHUNKS + 2)] + [range(CONV_CHUNKS + 2 * t, CONV_CHUNKS + 2 * t + 2) for t in range(1, TC)]
WEIGHTS_AROUND_CV1 += [range(CONV_CHUNKS + 2 * TC, WCHUNKS)]

BN_CV1, BN_M, BN_PROJ, BN_CV2 = 0, TC, TC + N * TH, TC + 2 * N * TH
NBN = 2 * TC + 2 * N * TH

def plan(last):
    def attention(n):
        jobs = [(kind, n, t) for t in range(TH) for kind in "qk"]
        return jobs + [(kind, n, t) for kind in ("v", "aot", "proj") for t in range(TH)]
    jobs = attention(0) + [("conv", 1, 0)] + ([] if last else [("stat0", 0, 0)]) + [("conv", 1, 1)] + attention(1)
    jobs += [("cv2", 0, t) for t in range(TC)]
    if not last:
        jobs += [("cv1", 0, t) for t in range(TC - 1)] + [("stat1", 0, 0), ("cv1", 0, TC - 1)]
        jobs += [("conv", 0, 0), ("tr", 0, 0), ("tr", 0, 1), ("conv", 0, 1), ("tr", 0, 2), ("tr", 0, 3)]
    else:
        jobs += [("stat1", 0, 0)] + [("tr", 0, t) for t in range(TC)]
    jobs += [("gram", 0, t) for t in range(TC // 2)]
    act = [j for j in jobs if j[0] not in ("stat0", "stat1", "gram")]
    return {j: i for i, j in enumerate(jobs)}, {j: i for i, j in enumerate(act)}


PLAN = {last: plan(last) for last in (False, True)}
JOBS, ACTS = len(PLAN[False][0]), len(PLAN[False][1])
FIRST_JOBS, FIRST_ACTS = 1 + TC + TH, TC + TH
STEPS = HEADS * NT
ATT = N * STEPS
RING = 3
TURN = 4
AHEAD = NT + TURN
PRIME = 4
AOT_STEP = STEPS - AHEAD + 2
DVE_LO = [6, 14] + [s for s in range(STEPS - AHEAD + 1, STEPS) if s % 2]
LO_STEPS = {"dve": DVE_LO, "pool": [s for s in range(STEPS) if s not in DVE_LO]}
SQUARINGS = 4
ROUNDS = 6
GROUP = 4
PER_ROUND_DVE = 2 * SQUARINGS + 2
PER_ROUND_PE = 4 * SQUARINGS + 1
DVE_SETUP_CHAIN = 35
DVE_IMAGE_CHAIN = 90
DVE_ROUND_CHAIN = 2


def spread(ap, dim, n):
    ap = ap.unsqueeze(dim)
    return ap.broadcast_to([n if i == dim else k for i, k in enumerate(ap.shape)])


def build(nc, x, w_all, bn, r_in, sel_in, consts, l1w, l1b, out):
    x1d = nc.dram_tensor("x1_scratch", (B, TC, P, HW), F32).ap()
    x_v = x.rearrange("b (t p) h w -> b t p (h w)", p=P)
    out_v = out.rearrange("b (t p) h w -> b t p (h w)", p=P)
    ctx = ExitStack()
    with ctx:
        def sb(name, shape, dt):
            return ctx.enter_context(nc.sbuf_tensor(name, shape, dt))

        def sem(name):
            return ctx.enter_context(nc.semaphore(name))

        WH = sb("w_hi", [P, W_END], F16)
        WL = sb("w_lo", [P, W_END], F16)
        X = sb("x_tiles", [P, TC, HW], F32)
        Y0 = sb("y0", [P, 2, TH, HW], F16)
        YP = sb("y_padded", [P, N + 1, 2, TH, PF, PF], F16)
        Z = sb("z", [P, 2, TH, HW], F16)
        SH = sb("shared", [P, TC, 2, HW], F16)
        QK3 = sb("q3_k2", [P, 2, HEADS, HW], F16)
        V = sb("v", [P, NT, HEADS, VW + 1], F16)
        R4 = sb("ring", [P, 4, HW], F32)
        AO = sb("attn_out", [P, NT, CH], F32)
        CST = sb("consts", [P, 4, P], F32)
        BNS = sb("bn_scale", [P, NBN], F32)
        BNB = sb("bn_bias", [P, NBN], F32)
        RHL = sb("positions", [P, N, TH, P], F16)
        SEL = sb("select", [P, HW], F16)
        LW = sb("l1_w", [P, TC], F32)
        LB = sb("l1_b", [P, TC], F32)
        HALFNEG = sb("minus_half", [P, NBN], F32)
        SHIFT = sb("shift", [P, 1], F32)
        BST = sb("bn_stats", [P, TC, 2, 6], F32)
        MV = sb("mean_var", [P, TC, 2], F32)
        ST = sb("mean_sq", [P, TC, 2], F32)
        GS = sb("group_mean_sq", [P, TC, 2], F32)
        VAR = sb("group_var", [P, TC], F32)
        RST = sb("rstd", [P, TC], F32)
        NB = sb("norm_bias", [P, TC], F32)
        NM = sb("minus_max", [P, HEADS * NT], F32)
        NMT = sb("minus_max_t", [NT, 2, P], F16)
        RC = sb("recip", [P, NT], F32)
        COV = sb("cov", [P, TC, P], F32)
        BNR = COV[:, 0, 0:4 * NBN].rearrange("p (k n) -> p k n", n=NBN)
        MU = sb("mu", [P, TC], F32)
        RSB = sb("rstd_of_images", [P, B + 1, TC], F32)
        NBB = sb("norm_bias_of_images", [P, B, TC], F32)

        ps = ctx.enter_context(nc.psum_tensor("ps", [P, 8, HALF], F32))

        def pair(j):
            return ps[:, 2 * (j % 4):2 * (j % 4) + 2, :].rearrange("p a n -> p (a n)")

        ident, avg16, ones64, ones = (CST[:, i, :] for i in range(4))
        XNH = AO[:, :, :].rearrange("p a c -> p (a c)").bitcast(F16).rearrange("p (t n) -> p t n", t=TC)
        XNL = Z[:, :, :, :].rearrange("p s t n -> p (s t) n")
        Q2 = SH[:, :, 0, :]
        K1 = SH[:, :, 1, :]
        Q3 = QK3[:, 0, :, :]
        K2 = QK3[:, 1, :, :]
        X1 = SH[:, :, :, :].rearrange("p t s n -> p t (s n)").bitcast(F32)
        YT_PARTS = [m.rearrange("p (t a c) -> p t a c", t=2, c=P) for m in (
            AO[:, :, :].rearrange("p a c -> p (a c)"), Q3.rearrange("p h n -> p (h n)").bitcast(F32))]

        def yt(t):
            return YT_PARTS[t // 2][:, t % 2, :, :]
        STAGE = X1
        A0 = SH[:, 0, :, :]

        def attended(hl, t):
            return A0[:, hl, :] if t == 0 else Z[:, hl, t, :]
        U = R4[:, 0:2, :]
        T = R4[:, 2:4, :]
        PF32 = R4[:, 0:RING, :]
        Z32 = Z[:, :, :, :].rearrange("p s t n -> p (s t n)").bitcast(F32).rearrange("p (r n) -> p r n", n=HW)
        PHL = [m.bitcast(F16).rearrange("p (s n) -> p s n", s=2) for m in (R4[:, RING, :], Z32[:, 0, :], Z32[:, 1, :])]

        def w2(Wt, base, k, width, lo, n):
            return Wt[:, base + k * width + lo:base + k * width + lo + n]

        wloaded = [sem(f"weights_loaded{i}") for i in range(4)]
        whigh = sem("weights_hi")
        wsplit = sem("weights_split")
        small_loaded = sem("small_loaded")
        setup_pool = sem("setup_pool")
        setup_dve = sem("setup_done")
        x_loaded = [sem(f"x_loaded{i}") for i in range(TC)]
        xn_ready = sem("xn_ready")
        xres_loaded = [sem(f"x_again{i}") for i in range(TC)]
        x1_stored = [sem(f"x1_stored{i}") for i in range(TC)]
        job_done = sem("job_done")
        act_done = sem("act_done")
        drained = sem("drained")
        stat_ready = sem("stat_ready")
        var_ready = sem("var_ready")
        x1_normed = sem("x1_normalised")
        dup_done = sem("doubles_done")
        rstd_ready = sem("rstd_ready")
        mx_done = sem("max_logits_done")
        mx_used = sem("max_taken")
        nmt_done = sem("max_transposed")
        nmt_ready = sem("max_row_ready")
        aug_loaded = sem("max_row_placed")
        qk_done = sem("logits_done")
        exp_done = sem("exp_done")
        ph_done = sem("p_hi_done")
        lo_done = {"pool": sem("p_lo_done_by_pool"), "dve": sem("p_lo_done_by_dve")}
        pv_done = sem("pv_done")
        o_used = sem("head_output_taken")
        chain = sem("dve_chain")
        l1_loaded = [sem(f"x1_loaded{i}") for i in range(GROUP * TC)]
        l1_stored = [sem(f"out_stored{i}") for i in range(4)]
        fin_pe = sem("fin_pe")
        fin_dve = sem("fin_dve")
        fin_stage = sem("fin_stage")
        fin_pool = sem("fin_pool")
        ap_done = sem("applied")
        ap_used = sem("applied_taken")
        mat_ready = sem("matrices_ready")
        fin_act = sem("fin_act")
        bn_read = sem("bn_loaded")
        bn_rstd = sem("bn_rstd")
        bn_ready = sem("bn_ready")

        block = ctx.enter_context(nc.Block())

        L1 = R4[:, :, :].rearrange("p r (t c) -> p r t c", t=8)
        BC = AO[:, :, :].rearrange("p a c -> p (a c)").rearrange("p (i t c) -> p i t c", i=4, t=4)
        Zf = Z[:, :, :, :].rearrange("p s t n -> p (s t n)").bitcast(F32).rearrange("p (i t c) -> p i t c", i=4, t=4)
        V4 = Y0[:, :, :, :].rearrange("p s t n -> p (s t n)").bitcast(F32)
        A_, Bm, Cm, W_ = (BC[:, i, :, :] for i in range(4))
        NY, NZ, NTm, SUB = (Zf[:, i, :, :] for i in range(4))
        SCR = L1[:, 0, 0:TC, :]
        SCR2 = L1[:, 1, 0:TC, :]
        I15 = L1[:, 2, 0, :]
        TR = V4[:, P:P + 8]
        IV = V4[:, P + 8:P + 16]
        DG = V4[:, P + 16:P + 24]
        EV = V4[:, P + 24:P + 40]
        CB = V4[:, P + 64:P + 64 + TC * B].rearrange("p (t b) -> p t b", t=TC)
        MB = V4[:, P + 128:P + 128 + TC * B].rearrange("p (t b) -> p t b", t=TC)
        LIN_H = WH[:, 0:8 * 2 * HW].bitcast(F32).rearrange("p (t n) -> p t n", n=HW)
        LIN_L = WL[:, 0:8 * 2 * HW].bitcast(F32).rearrange("p (t n) -> p t n", n=HW)

        def lin(i, t):
            return (LIN_H if i < GROUP // 2 else LIN_L)[:, (i % (GROUP // 2)) * TC + t, :]
        LOUT = X[:, :, :]
        SB = WH[:, 8 * 2 * HW:8 * 2 * HW + TC * 2 * P].bitcast(F32).rearrange("p (r c) -> p r c", c=P)

        def tiles(m):
            return m.rearrange("p (t c) -> p t c", c=P)

        def fin_pe_part(pe, mm):
            def blocks(dst, lhs, rhs):
                for t in range(TC):
                    ins = mm(dst[:, t * P:(t + 1) * P], lhs(t), rhs[:, t, :], start=True, stop=True)
                return ins

            def of(m):
                return lambda t: m[:, t, :]

            def all_ones(t):
                return ones
            pe.wait_ge(fin_stage, 1)
            blocks(pair(0), all_ones, SCR).then_inc(fin_pe, 1)
            pe.wait_ge(fin_stage, 2)
            mm(pair(1)[:, 0:TC], ones64, DG[:, 0:TC], start=True, stop=True).then_inc(fin_pe, 1)
            pe.wait_ge(fin_stage, 3)
            with pe.Fori(0, ROUNDS) as r:
                for k in range(SQUARINGS):
                    base = 3 + r * PER_ROUND_DVE + k * 2
                    pe.wait_ge(fin_stage, base)
                    pe.wait_ge(fin_act, 1 + r * 2 * SQUARINGS + 2 * k)
                    blocks(pair(1), of(NZ), NY).then_inc(fin_pe, 1)
                    blocks(pair(0), of(Bm), Bm).then_inc(fin_pe, 1)
                    blocks(pair(3), of(Cm), Cm).then_inc(fin_pe, 1)
                    pe.wait_ge(fin_stage, base + 1)
                    blocks(pair(2)[:, HALF:], of(NTm), NZ)
                    blocks(pair(1)[:, HALF:], of(NY), NTm).then_inc(fin_pe, 1)
                pe.wait_ge(fin_stage, 3 + r * PER_ROUND_DVE + 2 * SQUARINGS + 1)
                mm(pair(3)[:, 0:8], ones64, DG[:, 0:8], start=True, stop=True).then_inc(fin_pe, 1)
            last = 3 + ROUNDS * PER_ROUND_DVE
            pe.wait_ge(fin_stage, last + 1)
            mm(pair(3)[:, 0:8], ones64, DG[:, 0:8], start=True, stop=True).then_inc(fin_pe, 1)
            pe.wait_ge(fin_stage, last + 2)
            blocks(pair(0), all_ones, SCR).then_inc(fin_pe, 1)
            pe.wait_ge(fin_stage, last + 3)
            for t in range(TC):
                ins = mm(pair(1)[:, t * B:(t + 1) * B], SUB[:, t, :], MB[:, t, :], start=True, stop=True)
            ins.then_inc(fin_pe, 1)

        def count_drained(b, j, last):
            return b * JOBS + (PRIME + FIRST_JOBS + PLAN[last][0][j] + 1)

        def who(s):
            return "dve" if s in DVE_LO else "pool"

        def count_lo(b, n, s):
            steps = LO_STEPS[who(s)]
            return b * N * len(steps) + n * len(steps) + steps.index(s) + 1

        def count_done(b, j, last):
            return b * JOBS + (FIRST_JOBS + PLAN[last][0][j] + 1)

        def count_act(b, j, last):
            return b * ACTS + (FIRST_ACTS + PLAN[last][1][j] + 1)

        def count_stat(b, which, last):
            return b * 2 + (1 + (0 if last or which == 0 else 1) + 1)

        def place(j, last):
            if j[0] == "aot" and j[2] == 0:
                j = ("v", j[1], 0)
            return FIRST_JOBS + PLAN[last][0][j]

        def bank_pair(j, last=False):
            return pair(place(j, last))

        def turn_bank(n, h, last):
            e, f, _ = attention_pairs(n, last)
            return 2 * ((e if h else f) % 4)

        def attention_pairs(n, last):
            e = place(("v", n, 0), last)
            return e, e + 1, (e + 2, e + 3)

        @block.sync
        def _(sp):
            for dst, src in ((CST[:, :, :], consts), (BNR[:, :, :], bn), (R4[:, 0, 0:HALF], r_in),
                             (SEL[:, :], sel_in), (LW[:, :], l1w), (LB[:, :], l1b)):
                sp.dma_start(dst, src).then_inc(small_loaded, 16)
            for t in range(TC):
                sp.dma_start(X[:, t, :], x_v[0, t, :, :]).then_inc(x_loaded[t], 16)
            for c in range(WCHUNKS):
                if c >= 4:
                    sp.wait_ge(wsplit, c - 3)
                sp.dma_start(STAGE[:, c % 4, :], w_all[:, c * WCHUNK:(c + 1) * WCHUNK]).then_inc(wloaded[c % 4], 16)

            def image(b, last, following=None):
                if not last:
                    sp.wait_ge(xn_ready, following * TC)
                    for t in range(TC):
                        sp.dma_start(X[:, t, :], x_v[following, t, :, :]).then_inc(x_loaded[t], 16)
                for n in range(N):
                    for h in range(HEADS):
                        sp.wait_ge(nmt_ready, (b * N + n) * HEADS + h + 1)
                        sp.dma_start(Q3[HD:HD + 1, h, :], NMT[:, h % 2, :]).then_inc(aug_loaded, 16)
                sp.wait_ge(drained, count_drained(b, ("proj", 1, 1), last))
                for t in range(TC):
                    sp.dma_start(X1[:, t, :], x_v[b, t, :, :]).then_inc(xres_loaded[t], 16)
                for t in range(TC):
                    sp.wait_ge(drained, count_drained(b, ("cv2", 0, t), last))
                    sp.dma_start(x1d[b, t, :, :], X1[:, t, :]).then_inc(x1_stored[t], 16)

            with sp.Fori(1, B) as following:
                image(following - 1, False, following)
            image(B - 1, True)
            for t in range(TC):
                sp.wait_ge(x1_stored[t], 16 * B)
            with sp.Fori(0, B // GROUP) as g:
                for i in range(GROUP):
                    for t in range(TC):
                        sp.wait_ge(ap_used, g * GROUP * TC + i * TC + t + 1)
                        sp.dma_start(lin(i, t), x1d[g * GROUP + i, t, :, :]).then_inc(l1_loaded[i * TC + t], 16)
            for t in range(TC):
                sp.wait_ge(l1_stored[t], 16 * B + 16)

        @block.gpsimd
        def _(pool):
            g = nc.gpsimd
            g.memset(K2[HD:HD + 1, :, :], MSCALE).then_inc(setup_pool, 1)
            pool.wait_ge(setup_pool, 1)
            pool.wait_ge(bn_read, 1)
            g.tensor_tensor(BNS[:, :], BNR[:, 3, :], HALFNEG[:, :], ALU.pow).then_inc(bn_rstd, 1)
            pool.wait_ge(bn_rstd, 1)
            g.memset(YP[:, 0, :, :, :, :], 0.0).then_inc(setup_pool, 1)
            pool.wait_ge(setup_pool, 2)

            def rstds(count):
                pool.wait_ge(var_ready, count)
                g.tensor_tensor(RST[:, :], VAR[:, :], HALFNEG[:, 0:TC], ALU.pow).then_inc(rstd_ready, 1)

            def image(b, last):
                for n in range(N):
                    if n == 1 and not last:
                        rstds(count_stat(b, 0, last))
                    for s in LO_STEPS["pool"]:
                        pool.wait_ge(ph_done, count_lo(b, n, s))
                        g.tensor_tensor(PHL[s % RING][:, 1, :], PF32[:, s % RING, :], PHL[s % RING][:, 0, :], ALU.subtract)\
                            .then_inc(lo_done["pool"], 1)
                rstds(count_stat(b, 1, last))

            rstds(1)
            pool.wait_ge(rstd_ready, 1)
            for n in range(1, N + 1):
                g.memset(YP[:, n, :, :, :, :], 0.0).then_inc(setup_pool, 1)
                pool.wait_ge(setup_pool, n + 2)
            g.memset(V[:, :, :, :], 1.0).then_inc(setup_pool, 1)
            with pool.Fori(0, B - 1) as b:
                image(b, False)
            image(B - 1, True)
            pool.wait_ge(fin_dve, 1)
            g.tensor_tensor(EV[:, 8:16], EV[:, 0:8], HALFNEG[:, 0:8], ALU.pow).then_inc(fin_pool, 1)

        @block.scalar
        def _(act):
            a = nc.scalar
            def weights(chunks):
                for c in chunks:
                    act.wait_ge(wloaded[c % 4], 16 * (c // 4 + 1))
                    a.activation(WH[:, c * WCHUNK:(c + 1) * WCHUNK], STAGE[:, c % 4, :], ACT.Copy, scale=WSCALE)\
                        .then_inc(whigh, 1)

            def silu_of(i, done, free, col):
                act.wait_ge(job_done, done)
                act.wait_ge(drained, free)
                a.activation(U[:, i % 2, :], pair(i), ACT.Identity, bias=BNB[:, col:col + 1], scale=BNS[:, col:col + 1])
                a.activation(T[:, i % 2, :], pair(i), ACT.Tanh, bias=BNB[:, col:col + 1],
                             scale=BNS[:, col:col + 1]).then_inc(act_done, 1)

            def image(b, last):
                def silu_part(j, col):
                    silu_of(place(j, last), count_done(b, j, last), count_drained(b, j, last) - 2, col)

                def turned_max(n, h):
                    act.wait_ge(nmt_done, (b * N + n) * HEADS + h + 1)
                    a.activation(NMT[:, h % 2, :], ps[0:NT, turn_bank(n, h, last), 0:P], ACT.Copy, scale=1.0 / MSCALE)\
                        .then_inc(nmt_ready, 1)

                for n in range(N):
                    if n:
                        for t in range(TH):
                            silu_part(("conv", 1, t), BN_M + TH + t)
                    for t in range(TH):
                        for kind, dst in (("q", Q2), ("k", K1)):
                            j = (kind, n, t)
                            act.wait_ge(job_done, count_done(b, j, last))
                            for e in range(2):
                                r = slice(e * HD, (e + 1) * HD)
                                ins = a.activation(dst[r, 2 * t + e, :], bank_pair(j, last)[r, :], ACT.Copy,
                                                   scale=1.0 / WSCALE)
                            ins.then_inc(act_done, 1)
                            act.wait_ge(act_done, count_act(b, j, last))
                            for e in range(2):
                                r, o = slice(e * HD, (e + 1) * HD), slice((1 - e) * HD, (2 - e) * HD)
                                to = Q2[o, 2 * t + e, :] if kind == "q" else K2[0:HD, 2 * t + e, :]
                                ins = a.activation(to, dst[r, 2 * t + e, :], ACT.Copy)
                            ins.then_inc(dup_done, 1)
                    turned_max(n, 0)

                    def output_hi(t):
                        j = ("aot", n, t)
                        act.wait_ge(job_done, count_done(b, j, last))
                        a.activation(attended(0, t), bank_pair(j, last), ACT.Copy).then_inc(act_done, 1)
                    for t in range(2):
                        j = ("v", n, t)
                        act.wait_ge(job_done, count_done(b, j, last))
                        a.activation(V[:, 4 * t:4 * t + 4, :, 0:HD],
                                     bank_pair(j, last).rearrange("p (i h d) -> p i h d", i=4, h=HEADS), ACT.Copy,
                                     scale=1.0 / WSCALE).then_inc(act_done, 1)
                    for s in range(STEPS):
                        act.wait_ge(qk_done, b * ATT + n * STEPS + s + 1)
                        if s >= RING:
                            act.wait_ge(lo_done[who(s - RING)], count_lo(b, n, s - RING))
                        a.activation(PF32[:, s % RING, :], pair(attention_pairs(n, last)[2][s % 2]), ACT.Exp, bias=SHIFT[:, 0:1],
                                     scale=HD ** -0.5).then_inc(exp_done, 1)
                        if (s - 1) % NT == TURN and s - 1 + NT < STEPS:
                            turned_max(n, s // NT + 1)
                        if s == AOT_STEP + 2:
                            output_hi(0)
                    output_hi(1)
                    for t in range(TH):
                        silu_part(("proj", n, t), BN_PROJ + n * TH + t)
                for t in range(TC):
                    silu_part(("cv2", 0, t), BN_CV2 + t)
                if not last:
                    for t in range(TC):
                        silu_part(("cv1", 0, t), BN_CV1 + t)
                for t in range(TC):
                    if not last and t % 2 == 0:
                        silu_part(("conv", 0, t // 2), BN_M + t // 2)
                    j = ("tr", 0, t)
                    act.wait_ge(job_done, count_done(b, j, last))
                    a.activation(yt(t)[:, 0:NT // 2, :].rearrange("p a c -> p (a c)"),
                                 bank_pair(j, last)[:, 0:HALF], ACT.Copy).then_inc(act_done, 1)

            for t, chunks in enumerate(WEIGHTS_AROUND_CV1):
                weights(chunks)
                if t < TC:
                    act.wait_ge(bn_ready, 1)
                    silu_of(1 + t, t + 2, PRIME + t, BN_CV1 + t)
            for i in range(TC, TC + TH):
                silu_of(1 + i, i + 2, PRIME + i, BN_CV1 + i if i < TC else BN_M + i - TC)
            with act.Fori(0, B - 1) as b:
                image(b, False)
            image(B - 1, True)

            with act.Fori(0, ROUNDS) as r:
                for k in range(SQUARINGS):
                    done = 2 + r * PER_ROUND_PE + 4 * k
                    act.wait_ge(fin_pe, done + 2)
                    a.activation(Bm, tiles(pair(0)[:, 0:HALF]), ACT.Copy)
                    act.wait_ge(fin_pe, done + 3)
                    a.activation(Cm, tiles(pair(3)[:, 0:HALF]), ACT.Copy).then_inc(fin_act, 1)
                    act.wait_ge(fin_pe, done + 4)
                    a.activation(NZ, tiles(pair(2)[:, HALF:]), ACT.Copy).then_inc(fin_act, 1)
            with act.Fori(0, B) as b:
                for t in range(TC):
                    act.wait_ge(ap_used, b * TC + t + 1 + GROUP * TC)
                    act.dma_start(out_v[b, t, :, :], LOUT[:, t, :]).then_inc(l1_stored[t], 16)

        @block.tensor
        def _(pe):
            mm = nc.tensor.matmul

            def products(o, parts, rhs_of, first=True, final=True):
                end = len(parts) - 1
                for i, (w, key) in enumerate(parts):
                    for h in range(2):
                        ins = mm(o[:, h * HALF:(h + 1) * HALF], w, rhs_of(key, h), start=(first and i == 0),
                                 stop=(final and i == end))
                if final:
                    ins.then_inc(job_done, 1)

            def three(w_hi, w_lo, key):
                return [(w_hi, (0, key)), (w_hi, (1, key)), (w_lo, (0, key))]

            def cv1(o, t):
                parts = []
                for k in range(TC):
                    parts += three(w2(WH, W_CV1, k, C, t * P, P), w2(WL, W_CV1, k, C, t * P, P), k)
                products(o, parts, lambda key, h: (XNH, XNL)[key[0]][:, key[1], h * HALF:(h + 1) * HALF])

            def zr(key, h):
                return Z[:, key[0], key[1], h * HALF:(h + 1) * HALF]

            def conv(n, places, begin, have):
                for t in range(TH):
                    begin(t)

                    def shifted(key, h):
                        hl, (k, tap) = key
                        y0, dx = tap // 3 + h * (F // 2), tap % 3
                        return YP[:, n, hl, k, y0:y0 + F // 2, dx:dx + F]
                    for k in range(TH):
                        if t == 0:
                            have(k)
                        parts = []
                        for tap in range(TAPS):
                            base = W_M + (n * TAPS + tap) * TH * CH
                            parts += three(w2(WH, base, k, CH, t * P, P), w2(WL, base, k, CH, t * P, P), (k, tap))
                        products(places[t], parts, shifted, k == 0, k == TH - 1)
                    yield t

            def group_average(o):
                mm(o[:, 0:2 * TC], avg16, ST[:, :, :].rearrange("p t a -> p (t a)"), start=True, stop=True)\
                    .then_inc(job_done, 1)

            def module(b, n, last):
                def begin(j):
                    pe.wait_ge(drained, count_drained(b, j, last) - 4)

                mx_pair, out_pair, logit_pairs = attention_pairs(n, last)
                if n == 1:
                    for t in conv(1, [bank_pair(("conv", 1, t), last) for t in range(TH)],
                                  lambda t: begin(("conv", 1, t)),
                                  lambda k: pe.wait_ge(drained, count_drained(b, ("proj", 0, k), last))):
                        if t == 0 and not last:
                            begin(("stat0", 0, 0))
                            pe.wait_ge(stat_ready, count_stat(b, 0, last))
                            group_average(bank_pair(("stat0", 0, 0)))
                wq = W_QKV + n * TH * 3 * CH

                def qk(kind, t, ks):
                    m = t if kind == "q" else TH + t
                    parts = []
                    for k in ks:
                        parts += three(w2(WH, wq, k, 3 * CH, m * P, P), w2(WL, wq, k, 3 * CH, m * P, P), k)
                    if kind == "k" and ks[-1] == TH - 1:
                        parts.append((RHL[:, n, t, :], None))
                    products(bank_pair((kind, n, t), last), parts,
                             lambda key, h: SEL[:, h * HALF:(h + 1) * HALF] if key is None else zr(key, h),
                             ks[0] == 0, ks[-1] == TH - 1)

                early = [("q", 0), ("k", 0), ("q", 1)] if n else []
                if n == 0:
                    pe.wait_ge(drained, b * JOBS + (PRIME + FIRST_JOBS))
                else:
                    pe.wait_ge(drained, count_drained(b, ("conv", 1, 0), last))
                    for kind, t in early:
                        begin((kind, 1, t))
                        qk(kind, t, [0])
                    pe.wait_ge(drained, count_drained(b, ("conv", 1, 1), last))
                    for kind, t in early:
                        qk(kind, t, [1])
                for t in range(TH):
                    for kind in "qk":
                        if (kind, t) not in early:
                            begin((kind, n, t))
                            qk(kind, t, range(TH))
                pe.wait_ge(drained, count_drained(b, ("k", n, 0), last))
                pe.wait_ge(dup_done, (b * N + n) * 2 * TH + 2)

                def max_logits(m, o):
                    h, i = m // NT, m % NT
                    for e in range(2):
                        ins = mm(o[:, e * HALF:(e + 1) * HALF], Q2[:, h, i * P:(i + 1) * P],
                                 K1[:, h, e * HALF:(e + 1) * HALF], start=True, stop=True)
                    ins.then_inc(mx_done, 1)

                def turn_max(h, bank):
                    nc.tensor.transpose(ps[0:NT, bank, 0:P], NM[:, h * NT:(h + 1) * NT], ident).then_inc(nmt_done, 1)

                for m in range(NT):
                    if m >= 2:
                        pe.wait_ge(mx_used, b * ATT + n * STEPS + m - 1)
                    max_logits(m, pair((mx_pair, out_pair)[m % 2]))
                pe.wait_ge(mx_used, b * ATT + n * STEPS + NT)
                turn_max(0, turn_bank(n, 0, last))
                for t in range(2):
                    begin(("v", n, t))
                    if t == 1:
                        pe.wait_ge(nmt_ready, (b * N + n) * HEADS + 1)
                    for i in range(4):
                        pos = (4 * t + i) * P
                        o = bank_pair(("v", n, t), last)[:, i * CH:(i + 1) * CH]
                        for k in range(TH):
                            zh, zl = Z[:, 0, k, pos:pos + P], Z[:, 1, k, pos:pos + P]
                            vh, vl = w2(WH, wq, k, 3 * CH, 2 * CH, CH), w2(WL, wq, k, 3 * CH, 2 * CH, CH)
                            mm(o, zh, vh, start=(k == 0), stop=False)
                            mm(o, zh, vl, start=False, stop=False)
                            ins = mm(o, zl, vh, start=False, stop=(k == TH - 1))
                    ins.then_inc(job_done, 1)

                def logits(s):
                    h, i = s // NT, s % NT
                    keys = slice(i * P, (i + 1) * P)
                    if i == 0:
                        pe.wait_ge(aug_loaded, ((b * N + n) * HEADS + h + 1) * 16)
                    if s >= 2:
                        pe.wait_ge(exp_done, b * ATT + n * STEPS + s - 1)
                    o = pair(logit_pairs[s % 2])
                    for e in range(2):
                        mm(o[:, e * HALF:(e + 1) * HALF], K1[:, h, keys], Q2[:, h, e * HALF:(e + 1) * HALF],
                           start=True, stop=False)
                    for e in range(2):
                        ins = mm(o[:, e * HALF:(e + 1) * HALF], K2[0:HD + 1, h, keys],
                                 Q3[0:HD + 1, h, e * HALF:(e + 1) * HALF], start=False, stop=True)
                    ins.then_inc(qk_done, 1)

                def values(s):
                    h, i = s // NT, s % NT
                    pe.wait_ge(lo_done[who(s)], count_lo(b, n, s))
                    if i == 0:
                        pe.wait_ge(o_used, (b * N + n) * HEADS + h + 1)
                    vh1, vl, done = V[:, i, h, 0:HD + 1], V[:, i, h, HD + 1:VW], i == NT - 1
                    for q in range(NT):
                        o = pair(out_pair)[:, q * P:q * P + HD + 1]
                        ph = PHL[s % RING][:, 0, q * P:(q + 1) * P]
                        pl = PHL[s % RING][:, 1, q * P:(q + 1) * P]
                        mm(o, ph, vh1, start=(i == 0 and q % 4 == 0), stop=False, skip_group_check=True)
                        mm(o[:, 0:HD], ph, vl, start=False, stop=False, skip_group_check=True)
                        ins = mm(o, pl, vh1, start=False, stop=done, skip_group_check=True)
                    ins.then_inc(pv_done, 1)

                pe.wait_ge(drained, count_drained(b, ("k", n, 1), last))
                pe.wait_ge(dup_done, (b * N + n + 1) * 2 * TH)
                def turn_output(t):
                    for i in range(NT):
                        ins = nc.tensor.transpose(bank_pair(("aot", n, t), last)[:, i * P:(i + 1) * P],
                                                  AO[:, i, t * P:(t + 1) * P], ident)
                    ins.then_inc(job_done, 1)

                logits(0)
                logits(1)
                pe.wait_ge(drained, count_drained(b, ("v", n, 1), last))
                for m in range(NT, NT + 3):
                    if m == NT + 2:
                        pe.wait_ge(mx_used, b * ATT + n * STEPS + m - 1)
                    max_logits(m, pair((mx_pair, out_pair)[m % 2]))
                for s in range(STEPS):
                    if s + 2 < STEPS:
                        logits(s + 2)
                    if s:
                        values(s - 1)
                    if s == 0:
                        pe.wait_ge(mx_used, b * ATT + n * STEPS + AHEAD - 1)
                        max_logits(AHEAD - 1, pair(mx_pair))
                    if s + AHEAD <= STEPS:
                        pe.wait_ge(mx_used, b * ATT + n * STEPS + s + AHEAD)
                    if s % NT == TURN and s + NT < STEPS:
                        h = s // NT + 1
                        turn_max(h, turn_bank(n, h, last))
                        if s + AHEAD < STEPS:
                            pe.wait_ge(nmt_ready, (b * N + n) * HEADS + h + 1)
                    if s + AHEAD < STEPS:
                        max_logits(s + AHEAD, pair(mx_pair))
                    if s == AOT_STEP:
                        pe.wait_ge(nmt_ready, (b * N + n + 1) * HEADS)
                        pe.wait_ge(o_used, (b * N + n) * HEADS + 3)
                        turn_output(0)
                values(STEPS - 1)
                pe.wait_ge(o_used, (b * N + n + 1) * HEADS + 1)
                turn_output(1)
                wp = W_PROJ + n * TH * CH
                for k in range(TH):
                    pe.wait_ge(drained, count_drained(b, ("aot", n, k), last))
                    for t in range(TH):
                        products(bank_pair(("proj", n, t), last),
                                 three(w2(WH, wp, k, CH, t * P, P), w2(WL, wp, k, CH, t * P, P), k),
                                 lambda key, h: attended(*key)[:, h * HALF:(h + 1) * HALF], k == 0, k == TH - 1)

            def image(b, last):
                for n in range(N):
                    module(b, n, last)

                def begin(j):
                    pe.wait_ge(drained, count_drained(b, j, last) - 4)

                def joined(key, h):
                    hl, k = key
                    if k < TH:
                        return Y0[:, hl, k, h * HALF:(h + 1) * HALF]
                    y0 = 1 + h * (F // 2)
                    return YP[:, k // TH - 1, hl, k % TH, y0:y0 + F // 2, 1:1 + F]

                def cv2(t, ks):
                    parts = []
                    for k in ks:
                        parts += three(w2(WH, W_CV2, k, C, t * P, P), w2(WL, W_CV2, k, C, t * P, P), k)
                    products(bank_pair(("cv2", 0, t), last), parts, joined, ks[0] == 0, ks[-1] == (2 + N) * TH - 1)
                early = (1 + N) * TH
                for t in range(2):
                    begin(("cv2", 0, t))
                    cv2(t, range(early))
                for t in range(TH):
                    pe.wait_ge(drained, count_drained(b, ("proj", 1, t), last))
                    cv2(0, [early + t])
                cv2(1, range(early, early + TH))
                for t in range(2, TC):
                    begin(("cv2", 0, t))
                    cv2(t, range(early + TH))

                if not last:
                    pe.wait_ge(xn_ready, b * TC + 2 * TC)
                    for t in range(TC - 1):
                        begin(("cv1", 0, t))
                        cv1(bank_pair(("cv1", 0, t)), t)
                begin(("stat1", 0, 0))
                pe.wait_ge(stat_ready, count_stat(b, 1, last))
                group_average(bank_pair(("stat1", 0, 0), last))
                if not last:
                    begin(("cv1", 0, TC - 1))
                    cv1(bank_pair(("cv1", 0, TC - 1)), TC - 1)

                def turn_x1(tiles):
                    for t in tiles:
                        begin(("tr", 0, t))
                        pe.wait_ge(x1_normed, b * TC + t + 1)
                        for i in range(NT):
                            ins = nc.tensor.transpose(bank_pair(("tr", 0, t), last)[:, i * P:(i + 1) * P],
                                                      X1[:, t, i * P:(i + 1) * P], ident)
                        ins.then_inc(job_done, 1)
                if last:
                    turn_x1(range(TC))
                else:
                    for t in conv(0, [bank_pair(("conv", 0, t)) for t in range(TH)],
                                  lambda t: begin(("conv", 0, t)),
                                  lambda k: pe.wait_ge(drained, count_drained(b, ("cv1", 0, TH + k), last))):
                        turn_x1((2 * t, 2 * t + 1))
                for t in range(TC // 2):
                    begin(("gram", 0, t))
                    pe.wait_ge(drained, count_drained(b, ("tr", 0, 2 * t + 1), last))
                    for e in range(2):
                        for i in range(NT):
                            y = yt(2 * t + e)[:, i, :]
                            ins = mm(bank_pair(("gram", 0, t), last)[:, e * P:(e + 1) * P], y, y,
                                     start=(i == 0), stop=(i == NT - 1))
                    ins.then_inc(job_done, 1)

            pe.wait_ge(bn_read, 1)
            pe.wait_ge(stat_ready, 1)
            group_average(pair(0))
            pe.wait_ge(xn_ready, TC)
            pe.wait_ge(wsplit, TC * C // WCHUNK)
            for t in range(TC):
                if t == TC - 1:
                    pe.wait_ge(drained, PRIME + 1)
                cv1(pair(1 + t), t)
            pe.wait_ge(wsplit, CONV_CHUNKS)
            for t in conv(0, [pair(1 + TC + t) for t in range(TH)], lambda t: pe.wait_ge(drained, PRIME + 2 + t),
                          lambda k: pe.wait_ge(drained, PRIME + 1 + TH + k + 1)):
                pass
            pe.wait_ge(setup_dve, 1)
            with pe.Fori(0, B - 1) as b:
                image(b, False)
            image(B - 1, True)

            fin_pe_part(pe, mm)
            with pe.Fori(0, B // GROUP) as g:
                for i in range(GROUP):
                    for t in range(TC):
                        pe.wait_ge(l1_loaded[i * TC + t], 16 * g + 16)
                        pe.wait_ge(mat_ready, g * GROUP * TC + i * TC + t + 1)
                        for h in range(2):
                            ins = mm(pair(t)[:, h * HALF:(h + 1) * HALF], SB[:, t, :],
                                     lin(i, t)[:, h * HALF:(h + 1) * HALF], start=True, stop=True)
                        ins.then_inc(ap_done, 1)

        @block.vector
        def _(dve):
            v = nc.vector

            class Own:
                base, n = 0, 0

                def mark(self, ins):
                    ins.then_inc(chain, 1)
                    self.n += 1

                def wait(self):
                    dve.wait_ge(chain, self.base + self.n)

                def __call__(self, ins):
                    self.mark(ins)
                    self.wait()
            own = Own()

            def drain(ins):
                ins.then_inc(drained, 1)

            def split(hi, lo, src):
                own(v.tensor_copy(hi, src))
                return v.tensor_tensor(lo, src, hi, ALU.subtract)

            def stats(src, t):
                v.bn_stats(BST[:, t, 0, :], src[:, t, 0:HALF])
                return v.bn_stats(BST[:, t, 1, :], src[:, t, HALF:])

            def joined_stats():
                own.wait()
                v.memset(NB[:, 0:1], 0.0)
                for t in range(TC):
                    ins = v.bn_aggr(MV[:, t, :], BST[:, t, :, :].rearrange("p a s -> p (a s)"))
                own(ins)
                own(v.tensor_tensor(ST[:, :, 1:2], MV[:, :, 0:1], MV[:, :, 0:1], ALU.mult))
                v.tensor_copy(ST[:, :, 0:1], MV[:, :, 0:1])
                v.tensor_tensor(ST[:, :, 1:2], ST[:, :, 1:2], MV[:, :, 1:2], ALU.add).then_inc(stat_ready, 1)

            def image_stats(count):
                for t in range(TC):
                    dve.wait_ge(x_loaded[t], count)
                    own.mark(stats(X, t))
                joined_stats()

            def variances(o, count):
                dve.wait_ge(job_done, count)
                own(v.tensor_copy(GS[:, :, :].rearrange("p t a -> p (t a)"), o[:, 0:2 * TC]))
                drain(v.memset(NB[:, 0:1], 0.0))
                own(v.tensor_tensor(VAR[:, :].unsqueeze(2), GS[:, :, 0:1], GS[:, :, 0:1], ALU.mult))
                own(v.tensor_tensor(VAR[:, :].unsqueeze(2), GS[:, :, 1:2], VAR[:, :].unsqueeze(2), ALU.subtract))
                v.tensor_scalar(VAR[:, :], VAR[:, :], GN_EPS, None, ALU.add).then_inc(var_ready, 1)

            def norm_bias(count):
                dve.wait_ge(rstd_ready, count)
                own(v.scalar_tensor_tensor(NB[:, :].unsqueeze(2), GS[:, :, 0:1], -1.0, RST[:, :].unsqueeze(2), ALU.mult,
                                           ALU.mult))

            def normalised(src, t):
                return v.tensor_scalar(src[:, t, :], src[:, t, :], RST[:, t:t + 1], NB[:, t:t + 1], ALU.mult, ALU.add)

            def normalise_image():
                for t in range(TC):
                    own(normalised(X, t))
                    split(XNH[:, t, :], XNL[:, t, :], X[:, t, :]).then_inc(xn_ready, 1)

            def silu(i, count):
                dve.wait_ge(act_done, count)
                u = U[:, i % 2, :]
                own(v.scalar_tensor_tensor(u, T[:, i % 2, :], 1.0, u, ALU.add, ALU.mult))
                return u

            def padded(n, hl, t):
                return YP[:, n, hl, t, 1:1 + F, 1:1 + F]

            def square(m):
                return m.rearrange("p (y x) -> p y x", x=F)

            def cv1_out(t, u):
                if t < TH:
                    drain(split(Y0[:, 0, t, :], Y0[:, 1, t, :], u))
                else:
                    drain(split(padded(0, 0, t - TH), padded(0, 1, t - TH), square(u)))

            v.memset(RC[:, 0:1], 0.0).then_inc(drained, PRIME)
            v.memset(RC[:, 2:3], 0.0).then_inc(pv_done, RING)
            v.memset(RC[:, 3:4], 0.0).then_inc(o_used, 1)
            v.memset(RC[:, 4:5], 0.0).then_inc(fin_act, 1)
            v.memset(SHIFT[:, :], PSHIFT)
            v.memset(RSB[:, :, :], 0.0)
            v.memset(MU[:, :], 0.0)
            v.memset(HALFNEG[:, :], -0.5)
            dve.wait_ge(small_loaded, 6 * 16)
            v.tensor_scalar(BNR[:, 3, :], BNR[:, 3, :], BN_EPS, None, ALU.add).then_inc(bn_read, 1)
            image_stats(16)
            raw = R4[:, 0, 0:HALF].rearrange("p (n t c) -> p n t c", n=N, t=TH)
            own(v.tensor_scalar(RHL[:, :, :, :], raw, WSCALE, None, ALU.mult))
            own(v.scalar_tensor_tensor(RHL[HD:P, :, :, :], raw[HD:P, :, :, :], WSCALE, RHL[HD:P, :, :, :], ALU.mult,
                                       ALU.subtract))
            variances(pair(0), 1)
            dve.wait_ge(bn_rstd, 1)
            own(v.tensor_tensor(BNS[:, :], BNS[:, :], BNR[:, 0, :], ALU.mult))
            own(v.tensor_tensor(BNB[:, :], BNR[:, 2, :], BNS[:, :], ALU.mult))
            own(v.tensor_tensor(BNB[:, :], BNR[:, 1, :], BNB[:, :], ALU.subtract))
            v.tensor_scalar(BNB[:, :], BNB[:, :], 0.5, None, ALU.mult)
            v.tensor_scalar(BNS[:, :], BNS[:, :], 0.5 / WSCALE, None, ALU.mult).then_inc(bn_ready, 1)
            v.memset(COV[:, :, :], 0.0)
            norm_bias(1)
            normalise_image()
            dve.wait_ge(setup_pool, 2)
            for t, chunks in enumerate(WEIGHTS_AROUND_CV1):
                for c in chunks:
                    dve.wait_ge(whigh, c + 1)
                    v.scalar_tensor_tensor(WL[:, c * WCHUNK:(c + 1) * WCHUNK], STAGE[:, c % 4, :], WSCALE,
                                           WH[:, c * WCHUNK:(c + 1) * WCHUNK], ALU.mult, ALU.subtract)\
                        .then_inc(wsplit, 1)
                if t < TC:
                    cv1_out(t, silu(1 + t, t + 1))
            dve.wait_ge(setup_pool, N + 3)
            v.memset(NM[:, 0:1], 0.0).then_inc(setup_dve, 1)
            for t in range(TH):
                drain(split(Z[:, 0, t, :], Z[:, 1, t, :], silu(1 + TC + t, TC + t + 1)))
            assert own.n == DVE_SETUP_CHAIN, ("set-up", own.n)

            def image(b, last):
                def done(j):
                    dve.wait_ge(act_done, count_act(b, j, last))

                def silu_job(j):
                    return silu(place(j, last), count_act(b, j, last))

                def z_out(j):
                    drain(split(Z[:, 0, j[2], :], Z[:, 1, j[2], :], silu_job(j)))

                for n in range(N):
                    mx_pair, out_pair, _ = attention_pairs(n, last)
                    if n == 1:
                        if not last:
                            image_stats(b * 16 + 32)
                        for t in range(TH):
                            if t == 1 and not last:
                                variances(bank_pair(("stat0", 0, 0)), count_done(b, ("stat0", 0, 0), last))
                            z_out(("conv", 1, t))
                        if not last:
                            norm_bias(count_stat(b, 0, last))

                    def low_parts(kind, t):
                        j = (kind, n, t)
                        done(j)
                        for e in range(2):
                            r, o, h = slice(e * HD, (e + 1) * HD), slice((1 - e) * HD, (2 - e) * HD), 2 * t + e
                            hi = (Q2 if kind == "q" else K1)[r, h, :]
                            ins = v.scalar_tensor_tensor(Q3[0:HD, h, :] if kind == "q" else K1[o, h, :],
                                                         bank_pair(j, last)[r, :], 1.0 / WSCALE, hi, ALU.mult,
                                                         ALU.subtract)
                        drain(ins)

                    def take_max(m, o):
                        dve.wait_ge(mx_done, b * ATT + n * STEPS + m + 1)
                        v.tensor_reduce(NM[:, m:m + 1], o, AX.X, ALU.max, negate=True).then_inc(mx_used, 1)

                    low_parts("q", 0)
                    low_parts("k", 0)
                    for m in range(NT):
                        take_max(m, pair((mx_pair, out_pair)[m % 2]))
                    low_parts("q", 1)
                    low_parts("k", 1)
                    for t in range(2):
                        j = ("v", n, t)
                        done(j)
                        drain(v.scalar_tensor_tensor(V[:, 4 * t:4 * t + 4, :, HD + 1:VW],
                                                     bank_pair(j, last).rearrange("p (i h d) -> p i h d", i=4, h=HEADS),
                                                     1.0 / WSCALE, V[:, 4 * t:4 * t + 4, :, 0:HD], ALU.mult,
                                                     ALU.subtract))

                    for m in range(NT, NT + 2):
                        take_max(m, pair((mx_pair, out_pair)[m % 2]))

                    def head_output(h):
                        dve.wait_ge(pv_done, b * ATT + n * STEPS + (h + 1) * NT + RING)
                        o = pair(out_pair).rearrange("p (q d) -> p q d", d=P)
                        own(v.reciprocal(RC[:, :].unsqueeze(2), o[:, :, HD:HD + 1]))
                        v.tensor_tensor(AO[:, :, h * HD:(h + 1) * HD], o[:, :, 0:HD],
                                        spread(RC[:, :], 2, HD), ALU.mult).then_inc(o_used, 1)

                    def output_lo(t):
                        done(("aot", n, t))
                        drain(v.tensor_tensor(attended(1, t), bank_pair(("aot", n, t), last), attended(0, t),
                                              ALU.subtract))

                    for s in range(STEPS):
                        dve.wait_ge(exp_done, b * ATT + n * STEPS + s + 1)
                        dve.wait_ge(pv_done, b * ATT + n * STEPS + s + 1)
                        hi, lo, e = PHL[s % RING][:, 0, :], PHL[s % RING][:, 1, :], PF32[:, s % RING, :]
                        if s in DVE_LO:
                            split(hi, lo, e).then_inc(lo_done["dve"], 1)
                        else:
                            v.tensor_copy(hi, e).then_inc(ph_done, 1)
                        if s % NT == 1 and s > 1:
                            head_output(s // NT - 1)
                        if s < 2:
                            take_max(NT + 2 + s, pair(mx_pair))
                        if s and s - 1 + AHEAD < STEPS:
                            take_max(s - 1 + AHEAD, pair(mx_pair))
                        if s == AOT_STEP + 4:
                            output_lo(0)
                    head_output(HEADS - 1)
                    output_lo(1)
                    for t in range(TH):
                        u = square(silu_job(("proj", n, t)))
                        own(v.tensor_tensor(u, u, padded(n, 0, t), ALU.add))
                        own(v.tensor_tensor(u, u, padded(n, 1, t), ALU.add))
                        drain(split(padded(n + 1, 0, t), padded(n + 1, 1, t), u))
                if not last:
                    normalise_image()
                for t in range(TC):
                    u = silu_job(("cv2", 0, t))
                    dve.wait_ge(xres_loaded[t], b * 16 + 16)
                    drain(v.tensor_tensor(X1[:, t, :], X1[:, t, :], u, ALU.add))
                    own.wait()
                    dve.wait_ge(drained, count_drained(b, ("cv2", 0, t), last))
                    own.mark(stats(X1, t))
                joined_stats()
                if not last:
                    for t in range(TC - 1):
                        cv1_out(t, silu_job(("cv1", 0, t)))
                variances(bank_pair(("stat1", 0, 0), last), count_done(b, ("stat1", 0, 0), last))
                if not last:
                    cv1_out(TC - 1, silu_job(("cv1", 0, TC - 1)))
                norm_bias(count_stat(b, 1, last))
                v.tensor_copy(RSB[:, b, :], RST[:, :])
                v.tensor_copy(NBB[:, b, :], NB[:, :])
                mean = MV[:, :, 0:1].rearrange("p t a -> p (t a)")
                own(v.tensor_tensor(mean, mean, RST[:, :], ALU.mult))
                own(v.tensor_tensor(mean, mean, NB[:, :], ALU.add))
                v.tensor_tensor(MU[:, :], MU[:, :], mean, ALU.add)
                for t in range(TC):
                    dve.wait_ge(x1_stored[t], b * 16 + 16)
                    normalised(X1, t).then_inc(x1_normed, 1)
                for t in range(TC):
                    if not last and t % 2 == 0:
                        z_out(("conv", 0, t // 2))
                    done(("tr", 0, t))
                    drain(v.tensor_copy(yt(t)[:, NT // 2:, :].rearrange("p a c -> p (a c)"),
                                        bank_pair(("tr", 0, t), last)[:, HALF:]))
                for t in range(TC // 2):
                    dve.wait_ge(job_done, count_done(b, ("gram", 0, t), last))
                    cov = COV[:, 2 * t:2 * t + 2, :].rearrange("p t c -> p (t c)")
                    drain(v.tensor_tensor(cov, bank_pair(("gram", 0, t), last)[:, 0:2 * P], cov, ALU.add))

            with dve.Fori(0, B - 1) as b:
                own.base, own.n = b * DVE_IMAGE_CHAIN + DVE_SETUP_CHAIN, 0
                image(b, False)
                assert own.n == DVE_IMAGE_CHAIN, ("image", own.n)
            own.base, own.n = DVE_SETUP_CHAIN + (B - 1) * DVE_IMAGE_CHAIN, 0
            image(B - 1, True)

            own(v.memset(TR[:, :], 0.0))
            for t in range(TC):
                v.memset(TR[:, TC + t:TC + t + 1], 0.0).then_inc(l1_stored[t], 16)
            v.memset(TR[:, 0:1], 0.0).then_inc(ap_used, GROUP * TC)
            own(v.tensor_scalar(MU[:, :], MU[:, :], 1.0 / B, None, ALU.mult))
            own(v.tensor_scalar(I15, ident, 1.5, None, ALU.mult))

            def stage(ins):
                ins.then_inc(fin_stage, 1)

            def along(s, n=P):
                return spread(s, 2, n)

            def each(m):
                return spread(m, 1, TC)

            stage(v.tensor_tensor(SCR, each(ident), along(MU[:, :]), ALU.mult))
            dve.wait_ge(fin_pe, 1)
            own(v.tensor_tensor(W_, tiles(pair(0)[:, 0:HALF]), along(MU[:, :]), ALU.mult))
            own(v.scalar_tensor_tensor(A_, COV[:, :, :], 1.0 / (B * HW), W_, ALU.mult, ALU.subtract))
            own(v.tensor_tensor(A_, A_, each(ones64), ALU.mult))
            own(v.scalar_tensor_tensor(A_, each(ident), COV_EPS, A_, ALU.mult, ALU.add))
            own(v.tensor_tensor(SCR, A_, each(ident), ALU.mult))
            stage(v.tensor_reduce(DG[:, 0:TC], SCR, AX.X, ALU.add))
            dve.wait_ge(fin_pe, 2)
            own(v.tensor_copy(TR[:, 0:TC], pair(1)[:, 0:TC]))
            own(v.reciprocal(IV[:, 0:TC], TR[:, 0:TC]))
            own(v.tensor_tensor(Bm, A_, along(IV[:, 0:TC]), ALU.mult))
            own(v.scalar_tensor_tensor(Cm, Bm, -1.0, each(ident), ALU.mult, ALU.add))
            v.tensor_scalar(Cm, Cm, 1.0 / 64, None, ALU.mult)
            v.tensor_copy(NY, Bm)
            stage(v.tensor_copy(NZ, each(ident)))

            fin_chain = own.base + own.n
            with dve.Fori(0, ROUNDS) as r:
                own.base, own.n = fin_chain + r * DVE_ROUND_CHAIN, 0
                for k in range(SQUARINGS):
                    done = 2 + r * PER_ROUND_PE + 4 * k
                    dve.wait_ge(fin_pe, done + 1)
                    stage(v.scalar_tensor_tensor(NTm, tiles(pair(1)[:, 0:HALF]), -0.5, each(I15), ALU.mult, ALU.add))
                    dve.wait_ge(fin_pe, done + 4)
                    stage(v.tensor_copy(NY, tiles(pair(1)[:, HALF:])))
                dve.wait_ge(fin_act, 1 + r * 2 * SQUARINGS + 2 * SQUARINGS - 1)
                v.tensor_tensor(SCR, Bm, each(ident), ALU.mult)
                own(v.tensor_tensor(SCR2, Cm, each(ident), ALU.mult))
                v.tensor_reduce(DG[:, 0:TC], SCR, AX.X, ALU.add)
                stage(v.tensor_reduce(DG[:, TC:2 * TC], SCR2, AX.X, ALU.add))
                dve.wait_ge(fin_pe, 2 + (r + 1) * PER_ROUND_PE)
                own(v.reciprocal(IV[:, :], pair(3)[:, 0:2 * TC]))
                v.tensor_tensor(Bm, Bm, along(IV[:, 0:TC]), ALU.mult)
                stage(v.tensor_tensor(Cm, Cm, along(IV[:, TC:]), ALU.mult))
                assert own.n == DVE_ROUND_CHAIN, ("round", own.n)
            own.base, own.n = fin_chain + ROUNDS * DVE_ROUND_CHAIN, 0
            own(v.memset(EV[:, 0:1], 0.0))
            dve.wait_ge(fin_act, 1 + ROUNDS * 2 * SQUARINGS)
            pe_done = 2 + ROUNDS * PER_ROUND_PE
            own(v.tensor_tensor(SCR, A_, Bm, ALU.mult))
            own(v.tensor_reduce(DG[:, 0:TC], SCR, AX.X, ALU.add))
            own(v.tensor_tensor(SCR, A_, Cm, ALU.mult))
            stage(v.tensor_reduce(DG[:, TC:2 * TC], SCR, AX.X, ALU.add))
            dve.wait_ge(fin_pe, pe_done + 1)
            own(v.tensor_scalar(IV[:, 0:TC], pair(3)[:, TC:2 * TC], COV_EPS, None, ALU.is_le))
            own(v.tensor_scalar(IV[:, TC:], IV[:, 0:TC], -1.0, 1.0, ALU.mult, ALU.add))
            v.tensor_copy(EV[:, TC:2 * TC], TR[:, 0:TC])
            v.tensor_copy(EV[:, 0:TC], pair(3)[:, 0:TC]).then_inc(fin_dve, 1)
            dve.wait_ge(fin_pool, 1)
            own(v.tensor_tensor(DG[:, 0:TC], EV[:, 2 * TC:3 * TC], IV[:, TC:], ALU.mult))
            own(v.tensor_tensor(DG[:, TC:2 * TC], EV[:, 3 * TC:], IV[:, 0:TC], ALU.mult))
            own(v.tensor_tensor(W_, Bm, along(DG[:, 0:TC]), ALU.mult))
            own(v.tensor_tensor(SUB, NZ, along(DG[:, TC:2 * TC]), ALU.mult))
            own(v.tensor_tensor(SUB, SUB, W_, ALU.add))
            stage(v.tensor_tensor(SCR, each(ident), along(LW[:, :]), ALU.mult))
            for t in range(TC):
                v.tensor_scalar(MB[:, t, :], NBB[:, :, t], -1.0, MU[:, t:t + 1], ALU.mult, ALU.add)
            dve.wait_ge(fin_pe, pe_done + 2)
            own(v.tensor_tensor(SUB, tiles(pair(0)[:, 0:HALF]), SUB, ALU.mult))
            stage(v.memset(EV[:, 0:1], 0.0))
            dve.wait_ge(fin_pe, pe_done + 3)
            for t in range(TC):
                ins = v.tensor_scalar(CB[:, t, :], pair(1)[:, t * B:(t + 1) * B], -1.0, LB[:, t:t + 1], ALU.mult,
                                      ALU.add)
            own(ins)
            for t in range(TC):
                v.tensor_scalar(SB[:, t, :], SUB[:, t, :], RSB[:, 0, t:t + 1], None, ALU.mult).then_inc(mat_ready, 1)
            with dve.Fori(0, B // GROUP) as g:
                for i in range(GROUP):
                    for t in range(TC):
                        dve.wait_ge(ap_done, g * GROUP * TC + i * TC + t + 1)
                        dve.wait_ge(l1_stored[t], g * GROUP * 16 + i * 16 + 16)
                        v.scalar_tensor_tensor(LOUT[:, t, :], pair(t), CB[:, t, bass.ds(g * GROUP + i, 1)], lin(i, t),
                                               ALU.add, ALU.add).then_inc(ap_used, 1)
                        v.tensor_scalar(SB[:, t, :], SUB[:, t, :], RSB[:, g * GROUP + i + 1, t:t + 1], None,
                                        ALU.mult).then_inc(mat_ready, 1)


_INS = ("x", "w_all", "bn", "r", "sel", "consts", "l1w", "l1b")


def kernel(x, L0_conv_cv1_w, L0_conv_cv1_bn, L0_conv_cv2_w, L0_conv_cv2_bn, L0_conv_m_cv1_w, L0_conv_m_cv1_bn,
           L0_conv_m_qkv_w, L0_conv_m_rw, L0_conv_m_rh, L0_conv_m_cv2_w, L0_conv_m_cv2_bn, L1_conv_weight,
           L1_conv_bias):
    import numpy as np
    import concourse.bacc as bacc
    from concourse.bass_utils import run_bass_kernel_spmd

    def turned(w):
        o, i = w.shape
        return w.reshape(o, i // P, P).transpose(2, 1, 0).reshape(P, -1)

    cv1, cv2, mc, qkv, mp = (np.asarray(a) for a in (L0_conv_cv1_w, L0_conv_cv2_w, L0_conv_m_cv1_w, L0_conv_m_qkv_w,
                                                     L0_conv_m_cv2_w))
    parts = [turned(cv1[:, :, 0, 0])]
    parts += [turned(mc[n, :, :, tap // 3, tap % 3]) for n in range(N) for tap in range(TAPS)]
    parts += [turned(qkv[n, :, :, 0, 0]) for n in range(N)]
    parts += [turned(mp[n, :, :, 0, 0]) for n in range(N)]
    parts += [turned(cv2[:, :, 0, 0])]
    w_all = np.ascontiguousarray(np.concatenate(parts, axis=1))
    bn1, bn2, bm, bp = (np.asarray(a) for a in (L0_conv_cv1_bn, L0_conv_cv2_bn, L0_conv_m_cv1_bn, L0_conv_m_cv2_bn))
    bn = np.concatenate([bn1, bm.transpose(1, 0, 2).reshape(4, -1), bp.transpose(1, 0, 2).reshape(4, -1), bn2], axis=1)
    bn = np.ascontiguousarray(bn.reshape(4, NBN, P).transpose(2, 0, 1))

    rw, rh = (np.asarray(r).reshape(N, TH, P, F).transpose(3, 0, 1, 2) for r in (L0_conv_m_rw, L0_conv_m_rh))
    r = np.concatenate([rw, rh, rw, rh], axis=0).reshape(P, -1)
    row, pos = np.arange(F)[:, None], np.arange(HW)[None]
    sel = np.concatenate([pos % F == row, pos // F == row] * 2, axis=0).astype(np.float16)
    i = np.arange(P)
    consts = np.stack([np.eye(P), (i[:, None] // 16 == i[None] // 16) / 16.0, i[:, None] // 64 == i[None] // 64,
                       np.ones((P, P))], axis=1).astype(np.float32)
    arrays = dict(x=np.ascontiguousarray(x), w_all=w_all, bn=bn, r=np.ascontiguousarray(r), sel=sel,
                  consts=np.ascontiguousarray(consts),
                  l1w=np.ascontiguousarray(np.asarray(L1_conv_weight).reshape(TC, P).T),
                  l1b=np.ascontiguousarray(np.asarray(L1_conv_bias).reshape(TC, P).T))
    nc = bacc.Bacc("TRN2", target_bir_lowering=False, num_devices=1)
    args = [nc.dram_tensor("in_" + k, arrays[k].shape, mybir.dt.from_np(arrays[k].dtype), kind="ExternalInput").ap() for k in _INS]
    out = nc.dram_tensor("out", (B, C, F, F), F32, kind="ExternalOutput").ap()
    build(nc, *args, out)
    ran = run_bass_kernel_spmd(nc, [{"in_" + k: arrays[k] for k in _INS}], core_ids=[0])
    return ran.results[0]["out"]
```
